# Optimizing a Trainium2 kernel written in Bass

```python
import numpy as np
import jax
import jax.numpy as jnp

def _softmax(x, axis=-1):
    return jax.nn.softmax(x, axis=axis)

def _gelu(x):
    return jax.nn.gelu(x, approximate=True)

def _silu(x):
    return jax.nn.silu(x)

def _sigmoid(x):
    return jax.nn.sigmoid(x)

def _layernorm(x, axis=-1, eps=1e-05):
    m = jnp.mean(x, axis=axis, keepdims=True)
    v = jnp.var(x, axis=axis, keepdims=True)
    return (x - m) / jnp.sqrt(v + eps)

def _scatter_add(tgt, idx, src, axis=0):
    return tgt.at[idx].add(src)

def _segment_sum(src, seg, n):
    return jax.ops.segment_sum(src, seg, n)
kernel_name = 'mk_gnn_resnorm_d4_gnn_r32_4a254e'

def setup_inputs(seed: int=0):
    np.random.seed(seed)
    _w = jnp.asarray

    def _rec_inputs():
        import jax
        import jax.numpy as jnp
        _gk = jax.random.key(seed)
        x = -0.0005121 + 1.001 * jax.random.normal(jax.random.fold_in(_gk, 1), (3125, 64), jnp.float32)
        _s = jax.random.randint(jax.random.fold_in(_gk, 2), (50000,), 0, 3125, jnp.int32)
        _d = jax.random.randint(jax.random.fold_in(_gk, 3), (50000,), 0, 3125, jnp.int32)
        _loop = jnp.arange(3125, dtype=jnp.int32)
        src = jnp.concatenate([_s, _d, _loop])
        dst = jnp.concatenate([_d, _s, _loop])
        _o = jnp.argsort(dst, stable=True)
        src = src[_o]
        dst = dst[_o]
        edge_type_16 = jax.random.randint(jax.random.fold_in(_gk, 13), (103125,), 0, 16, jnp.int32)
        edge_weight = jax.random.uniform(jax.random.fold_in(_gk, 14), (103125,), jnp.float32, 0.0, 0.999999)
        return (x, src, dst, edge_type_16, edge_weight)
    x, src, dst, edge_type_16, edge_weight = _rec_inputs()

    def _L0_gnn_setup():
        import jax, jax.numpy as jnp
        import numpy as np
        N_NODES = 50000
        N_EDGES = 25000
        D_IN = 64
        D_OUT = 64
        NUM_RELS = 16
        key = jax.random.key(seed)
        k1, k2, k3, k4, k5 = jax.random.split(key, 5)
        feat = jax.random.normal(k1, (N_NODES, D_IN), dtype=jnp.float32)
        weight = jax.random.normal(k2, (NUM_RELS, D_IN, D_OUT), dtype=jnp.float32) * 0.05
        src = jax.random.randint(k3, (N_EDGES,), 0, N_NODES, dtype=jnp.int32)
        dst = jax.random.randint(k4, (N_EDGES,), 0, N_NODES, dtype=jnp.int32)
        etypes = jax.random.randint(k5, (N_EDGES,), 0, NUM_RELS, dtype=jnp.int32)
        return {'feat': feat, 'weight': weight, 'src': src, 'dst': dst, 'etypes': etypes}
    _L0_gnn_all = _L0_gnn_setup()
    _L0_gnn_in = {k: v for k, v in _L0_gnn_all.items() if k in ('weight',)}
    del _L0_gnn_all

    def _L1_gnn_setup():
        import jax, jax.numpy as jnp
        import numpy as np
        N_NODES = 3125
        N_EDGES = 50000
        F_IN = 64
        F_OUT = 64
        key = jax.random.key(seed)
        k1, k2, k3, k4 = jax.random.split(key, 4)
        x = jax.random.normal(k1, (N_NODES, F_IN), dtype=jnp.float32)
        edge_index = jax.random.randint(k2, (2, N_EDGES), 0, N_NODES, dtype=jnp.int64)
        lim = 1.0 / np.sqrt(2 * F_IN)
        W = jax.random.uniform(k3, (F_OUT, 2 * F_IN), minval=-lim, maxval=lim, dtype=jnp.float32)
        b = jax.random.uniform(k4, (F_OUT,), minval=-lim, maxval=lim, dtype=jnp.float32)
        return {'x': x, 'edge_index': edge_index, 'num_nodes': N_NODES, 'W': W, 'b': b}
    _L1_gnn_all = _L1_gnn_setup()
    _L1_gnn_in = {k: v for k, v in _L1_gnn_all.items() if k in ('W', 'b')}
    del _L1_gnn_all

    def _L2_gnn_setup():
        import jax, jax.numpy as jnp
        import numpy as np
        N_NODES = 50000
        N_EDGES = 50000
        N_FEAT = 64
        key = jax.random.key(seed)
        k1, k2, k3 = jax.random.split(key, 3)
        x = jax.random.normal(k1, (N_NODES, N_FEAT), dtype=jnp.float32)
        edge_index = jax.random.randint(k2, (2, N_EDGES), 0, N_NODES, dtype=jnp.int64)
        edge_weights = jax.random.uniform(k3, (N_EDGES,), dtype=jnp.float32)
        return {'x': x, 'edge_index': edge_index, 'edge_weights': edge_weights}
    _L2_gnn_all = _L2_gnn_setup()
    _L2_gnn_in = {k: v for k, v in _L2_gnn_all.items() if k in ()}
    del _L2_gnn_all

    def _L3_gnn_setup():
        import jax, jax.numpy as jnp
        import numpy as np
        N_NODES = 50000
        IN_FT = 64
        OUT_FT = 64
        J = 3
        MAX_SCALE = 2 ** (J - 1)
        TOTAL_DIM = IN_FT * (1 + (J - 1) + J * (J - 1) // 2)
        N_EDGES = 25000
        key = jax.random.key(seed)
        k1, k2, k3, k4, k5 = jax.random.split(key, 5)
        seq = jax.random.normal(k1, (N_NODES, IN_FT), dtype=jnp.float32)
        edge_index = jax.random.randint(k2, (2, N_EDGES), 0, N_NODES, dtype=jnp.int32)
        edge_weight = jax.random.uniform(k3, (N_EDGES,), dtype=jnp.float32)
        std = 1.414 * np.sqrt(2.0 / (OUT_FT + TOTAL_DIM))
        fc_w = jax.random.normal(k4, (OUT_FT, TOTAL_DIM), dtype=jnp.float32) * std
        bias = jnp.zeros((OUT_FT,), dtype=jnp.float32)
        prelu_a = jnp.array(0.25, dtype=jnp.float32)
        return {'seq': seq, 'edge_index': edge_index, 'edge_weight': edge_weight, 'fc_w': fc_w, 'bias': bias, 'prelu_a': prelu_a}
    _L3_gnn_all = _L3_gnn_setup()
    _L3_gnn_in = {k: v for k, v in _L3_gnn_all.items() if k in ('fc_w', 'bias', 'prelu_a')}
    del _L3_gnn_all
    return {'x': x, 'src': src, 'dst': dst, 'edge_type_16': edge_type_16, 'edge_weight': edge_weight, 'L0_gnn_weight': _L0_gnn_in['weight'], 'L1_gnn_W': _L1_gnn_in['W'], 'L1_gnn_b': _L1_gnn_in['b'], 'L3_gnn_fc_w': _L3_gnn_in['fc_w'], 'L3_gnn_bias': _L3_gnn_in['bias'], 'L3_gnn_prelu_a': _L3_gnn_in['prelu_a']}

def reference(x, src, dst, edge_type_16, edge_weight, L0_gnn_weight, L1_gnn_W, L1_gnn_b, L3_gnn_fc_w, L3_gnn_bias, L3_gnn_prelu_a):
    import jax
    import jax.numpy as jnp

    def _L0_gnn_ref(feat, weight, src, dst, etypes):
        import jax, jax.numpy as jnp
        import numpy as np
        N_NODES = 50000
        N_EDGES = 25000
        D_IN = 64
        D_OUT = 64
        NUM_RELS = 16
        num_rels = weight.shape[0]
        h_src = feat[src]
        msg = jnp.zeros((h_src.shape[0], weight.shape[2]), dtype=feat.dtype)
        for r in range(num_rels):
            mask = etypes == r
            msg = msg + h_src * mask[:, None].astype(feat.dtype) @ weight[r]
        out = jax.ops.segment_sum(msg, dst, num_segments=feat.shape[0])
        return out

    def _L1_gnn_ref(x, edge_index, num_nodes, W, b):
        import jax, jax.numpy as jnp
        import numpy as np
        N_NODES = 3125
        N_EDGES = 50000
        F_IN = 64
        F_OUT = 64
        src = edge_index[0]
        dst = edge_index[1]
        agg = jax.ops.segment_sum(x[src], dst, num_segments=num_nodes)
        deg = jax.ops.segment_sum(jnp.ones((edge_index.shape[1],), dtype=x.dtype), dst, num_segments=num_nodes)
        agg = agg / jnp.maximum(deg, 1.0)[:, None]
        h = jnp.concatenate([agg, x], axis=-1)
        out = h @ W.T + b
        return out

    def _L2_gnn_ref(x, edge_index, edge_weights):
        import jax, jax.numpy as jnp
        import numpy as np
        N_NODES = 50000
        N_EDGES = 50000
        N_FEAT = 64
        src = edge_index[0]
        tgt = edge_index[1]
        messages = x[src] * edge_weights[:, None]
        out = jax.ops.segment_sum(messages, tgt, num_segments=x.shape[0])
        return out

    def _L3_gnn_ref(seq, edge_index, edge_weight, fc_w, bias, prelu_a):
        import jax, jax.numpy as jnp
        import numpy as np
        N_NODES = 50000
        IN_FT = 64
        OUT_FT = 64
        J = 3
        MAX_SCALE = 2 ** (J - 1)
        TOTAL_DIM = IN_FT * (1 + (J - 1) + J * (J - 1) // 2)
        N_EDGES = 25000
        n = seq.shape[0]
        f = seq.shape[1]
        src, dst = (edge_index[0], edge_index[1])

        def spmm(x):
            return jax.ops.segment_sum(x[src] * edge_weight[:, None], dst, num_segments=n)
        diff_list = []
        x_curr = seq
        for step in range(1, MAX_SCALE + 1):
            x_curr = spmm(x_curr)
            if step & step - 1 == 0:
                diff_list.append(x_curr)
        F0 = diff_list[-1]
        F1 = jnp.concatenate([jnp.abs(diff_list[i - 1] - diff_list[i]) for i in range(1, len(diff_list))], axis=1)
        U = jnp.concatenate(diff_list, axis=1)
        U_diff = [U]
        for _ in range(1, MAX_SCALE):
            U_diff.append(spmm(U_diff[-1]))
        feats2 = []
        for j in range(J):
            for jp in range(j + 1, J):
                s, e = (j * f, (j + 1) * f)
                feats2.append(jnp.abs(U_diff[jp][:, s:e] - U_diff[jp - 1][:, s:e]))
        F2 = jnp.concatenate(feats2, axis=1)
        feats = jnp.concatenate([F0, F1, F2], axis=1)
        out = feats @ fc_w.T + bias
        return jnp.where(out > 0, out, prelu_a * out)
    edge_index = jnp.stack([src, dst])
    x = _layernorm(x + _L0_gnn_ref(x, L0_gnn_weight, src, dst, edge_type_16), axis=-1)
    x = _layernorm(x + _L1_gnn_ref(x, edge_index, 3125, L1_gnn_W, L1_gnn_b), axis=-1)
    x = _layernorm(x + _L2_gnn_ref(x, edge_index, edge_weight), axis=-1)
    x = _layernorm(x + _L3_gnn_ref(x, edge_index, edge_weight, L3_gnn_fc_w, L3_gnn_bias, L3_gnn_prelu_a), axis=-1)
    return x

_drawn_inputs = setup_inputs


def setup_inputs(seed=0):
    import zlib

    import numpy as np

    out = dict(_drawn_inputs(seed))
    spreads = {'L3_gnn_bias': (0.0, 0.1)}
    factors = {}
    for name, (base, spread) in spreads.items():
        noise = np.random.default_rng([zlib.crc32(name.encode()), seed]).standard_normal(out[name].shape)
        drawn = base * np.exp(spread * noise) if base else spread * noise
        out[name] = jnp.asarray(drawn.astype(out[name].dtype))
    for name, factor in factors.items():
        out[name] = (out[name] * factor).astype(out[name].dtype)
    return out
```

```python
import concourse.bass as bass
import concourse.mybir as mybir
from contextlib import ExitStack

F32 = mybir.dt.float32
BF16 = mybir.dt.bfloat16
I32 = mybir.dt.int32
ALU = mybir.AluOpType
ACT = mybir.ActivationFunctionType
AX = mybir.AxisListType

P = 128
N = 3125
E = 103125
F = 64
RELS = 16
EPS = 1e-5

CH = -(-N // P)
LAST = N - (CH - 1) * P
TILES = -(-E // P)
TG = -(-TILES // P)
TP = TG * P
FULL_G = E // (P * P)
REST_T = (E - FULL_G * P * P) // P
REST_E = E - (FULL_G * P + REST_T) * P

WIN = 10
WC = WIN * CH
WS = WC + 2
TPW = 4
STEPS = CH
WPS = -(-CH * P // (STEPS * WIN))
WINS = STEPS * WPS
BLK = WPS * WIN
TPC = 35
GG = 7
XT = 8
XC = 16
RC = 3 * P
SLOT = [j % 3 for j in range(WPS - 1)] + [1]
AFTER = [[] for _ in range(2)] + [list(range(TPC * j // (WPS - 2), TPC * (j + 1) // (WPS - 2))) for j in range(WPS - 2)]
DB = WPS - 2
assert TPC % GG == 0 and WPS % 3 == 1 and WINS + STEPS <= RC and TILES + XC + TPC < TP

YB = 4
GB = 3
GROUPS = -(-STEPS // GB)
GN = GB * BLK
LASTB = STEPS - (GROUPS - 1) * GB
COLS = STEPS * BLK
CG = 5
CI = CH // CG
SL = CI * BLK
D1 = F + 1


def build(nc, x_in, src_in, dst_in, type_in, weight_in, rel_w, l1_w, l1_b, fc_w, fc_b, prelu_a, out):
    with ExitStack() as ctx:
        def sb(name, shape, dt=F32):
            return ctx.enter_context(nc.sbuf_tensor(name, shape, dt))

        def sem(name):
            return ctx.enter_context(nc.semaphore(name))

        class Arena:

            def __init__(self, name, size):
                self.size, self.at = size, 0
                self.tensor = sb(name, [P, size // 4])

            def restart(self):
                self.at = 0

            def take(self, shape, dt=F32):
                count = 1
                for n in shape[1:]:
                    count *= n
                words = -(-count * (2 if dt == BF16 else 4) // 4)
                a = self.tensor[0:shape[0], self.at // 4:self.at // 4 + words]
                self.at += 4 * words
                assert self.at <= self.size, (self.at, self.size)
                a = a if dt == F32 else a.bitcast(dt)
                if len(shape) == 3:
                    a = a.rearrange("p (a b) -> p a b", b=shape[2])
                if len(shape) == 4:
                    a = a.rearrange("p (a b c) -> p a b c", b=shape[2], c=shape[3])
                if len(shape) == 5:
                    a = a.rearrange("p (a b c d) -> p a b c d", b=shape[2], c=shape[3], d=shape[4])
                return a

        prep = Arena("prep_then_blocks_then_ring", 2 * CG * GB * SL * 4 + P * 4)
        loop = Arena("loop_then_dense", 9 * CH * F * 4 + CH * 2 * F * 4 + 2 * 512 * 4)

        y_dram = nc.dram_tensor("rel_rows", (CH * P * RELS, F), F32, kind="Internal").ap()

        def matrix(name):
            return (nc.dram_tensor(name, (GROUPS - 1, CG, P, GB * SL), F32, kind="Internal").ap(),
                    nc.dram_tensor(name + "_last", (CG, P, LASTB * SL), F32, kind="Internal").ap())

        weights_t, counts_t = matrix("weights_t"), matrix("counts_t")
        range_dram = nc.dram_tensor("ranges", (6, P), F32, kind="Internal").ap()


        ident = sb("ident", [P, P])
        ident2 = sb("ident2", [P, F])
        iota_b = sb("iota_b", [P, 256], BF16)
        iota_f = sb("iota_f", [P, P])
        win_base = sb("win_base", [P, WINS])
        chunk_base = sb("chunk_base", [P, STEPS])
        tile_no = sb("tile_no", [P, TG])
        tile_left = sb("tile_left", [P, TG])
        wa2_t = sb("wa2_t", [P, F])
        wb_t = sb("wb_t", [F, F])
        fc_t = sb("fc_t", [P, 3, F])
        ones_row = sb("ones_row", [1, P])
        small = sb("small", [P, 2 * F + 1])
        src_i = prep.take([P, TG, P], I32)
        dst_i = prep.take([P, TG, P], I32)
        typ_i = prep.take([P, TG, P], I32)
        tmp_i = prep.take([P, TG, P], I32)
        hi_i = typ_i
        w_f = prep.take([P, TG, P])
        dst_f = prep.take([P, TG, P])
        lo_f = prep.take([P, TG, P])
        key_f = prep.take([P, TG, P])
        gid_f = prep.take([P, TG, P])
        scr_f = prep.take([P, TG, P])
        scr2_f = prep.take([P, TG, P])
        t_min = sb("t_min", [P, TG])
        t_max = sb("t_max", [P, TG])
        has_a = prep.tensor[:, 0:TG * RC].rearrange("p (a b) -> p a b", b=RC)
        assert RC <= 3 * P
        has = prep.take([P, TG, RC])
        best = prep.take([P, 2, 2, RC])
        first_dst = sb("first_dst", [P, RC])
        last_dst = sb("last_dst", [P, RC])
        range_red = sb("range_red", [P, 2, 3])
        range_t = sb("range_t", [6, P])
        e_all = loop.take([P, TP, 3])
        e_dst = loop.take([P, TP])
        e_gid = loop.take([P, TP], I32)
        r_red = prep.take([1, 2, RC])
        r_a, r_lo, r_k, r_ex, r_zero, r_cum = [prep.take([1, RC]) for _ in range(6)]
        r_ki = prep.take([1, RC], I32)
        tab_lo = sb("tab_lo", [1, RC], I32)
        tab_ex = sb("tab_ex", [1, RC], I32)
        tab_cum = sb("tab_cum", [1, RC], I32)
        tab_any = sb("tab_any", [1, STEPS], I32)
        e_stage = sb("e_stage", [P, WPS, TPW * 3])
        sel_f = loop.take([P, 3, TPW, P])
        sel_b = loop.take([P, 3, TPW, P], BF16)
        key_b = loop.take([P, 3, TPW, WS], BF16)
        key_w = loop.take([P, 3, TPW, WC])
        dst_stage = loop.take([P, TPC])
        dsel = loop.take([P, TPC, P])
        slots_end, loop.at = loop.at, 5 * TP * 4
        xt = loop.take([F, CH * P])
        rel_sb = loop.take([F, RELS, F])
        l1_rows = loop.take([F, 3, F])
        fc_rows = loop.take([F, 6 * F])
        small_row = loop.take([1, 2 * F + 1])
        y_rows = loop.take([P, YB, RELS * F])
        loop.at = max(loop.at, slots_end)
        prep.restart()
        stage = prep.take([P, 2, 2, CH, BLK])
        x_sel_f = prep.take([P, XT, P])
        x_sel_b = prep.take([P, XT, P], BF16)
        x_key_b = prep.take([P, XT, WS], BF16)
        x_key_w = prep.take([P, XT, WS])
        x_dsel = prep.take([P, XC, P])
        gathered = sb("gathered", [P, TPC, D1])
        gid_stage = sb("gid_stage", [P, TPC], I32)
        x_gathered = sb("x_gathered", [P, XC, D1])
        x_gid_stage = sb("x_gid_stage", [P, XC], I32)
        accs = Arena("sums_then_product", max((2 * STEPS + 1) * D1, COLS) * 4)
        acc = accs.take([P, 1 + STEPS, D1])
        acc2 = accs.take([P, STEPS, D1])
        x0 = sb("x0", [P, CH, F])
        prep.restart()
        ring = prep.take([P, 2 * CG, GB * SL])
        y_t = accs.tensor[:, 0:COLS]

        loop.restart()
        ln_h, ln_c, ln_q, x1, x2, x3, u1, u2, u3 = [loop.take([P, CH, F]) for _ in range(9)]
        feats = loop.take([P, CH, 2, F])
        feats_t = loop.take([P, 2, 512])
        x1t = feats[0:F, :, :, :].rearrange("p c i f -> p (c i f)")
        ln_m = sb("ln_m", [P, 4, CH])
        ln_s = sb("ln_s", [P, 4, CH])
        ln_v = sb("ln_v", [P, 4, CH])
        ln_d = sb("ln_d", [P, 4, CH])
        ln_r = sb("ln_r", [P, 4, CH])
        deg = sb("deg", [P, CH])
        rdeg = sb("rdeg", [P, CH])

        ps = ctx.enter_context(nc.psum_tensor("ps", [P, 8, 512], F32))

        pads_set = sem("pads_set")
        main_loaded = [sem(f"loaded_{n}") for n in ("src", "dst", "typ", "w")]
        x_loaded = sem("x_loaded")
        x_tail_zero = sem("x_tail_zero")
        rel_loaded = sem("rel_loaded")
        w_loaded = sem("w_loaded")
        consts_made = sem("consts_made")
        consts_step = sem("consts_step")
        dve_step = sem("dve_step")
        xt_put = sem("xt_put")
        xt_copied = sem("xt_copied")
        y_put = sem("y_put")
        y_copied = sem("y_copied")
        y_stored = [sem(f"y_stored_{i}") for i in range(YB)]
        small_put = sem("small_put")
        small_copied = sem("small_copied")
        edges_ready = sem("edges_ready")
        edges_put = sem("edges_put")
        edges_copied = sem("edges_copied")
        best_ready = sem("best_ready")
        best_put = sem("best_put")
        range_ready = sem("range_ready")
        range_put = sem("range_put")
        range_turned = sem("range_turned")
        range_stored = sem("range_stored")
        range_back = sem("range_back")
        tables_ready = sem("tables_ready")
        staged = sem("staged")
        self_ready = sem("self_ready")
        sel_ready = sem("sel_ready")
        selb_ready = sem("selb_ready")
        keyw_ready = sem("keyw_ready")
        win_done = sem("win_done")
        win_out = sem("win_out")
        step_done = sem("step_done")
        blk_free = sem("blk_free")
        blk_stored = sem("blk_stored")
        xb_ready = sem("xb_ready")
        xs_ready = sem("xs_ready")
        x_done = sem("x_done")
        x_added = sem("x_added")
        ids_staged = sem("ids_staged")
        row_landed = [sem(f"row_landed_{s}") for s in range(TPC)]
        dst_staged = sem("dst_staged")
        dsel_ready = sem("dsel_ready")
        rel_done = sem("rel_done")
        rel_out = sem("rel_out")
        x_ids_staged = sem("x_ids_staged")
        x_row_landed = [sem(f"x_row_landed_{s}") for s in range(XC)]
        xd_ready = sem("xd_ready")
        xd_done = sem("xd_done")
        xd_added = sem("xd_added")
        landed = [sem(f"slice_landed_{s}") for s in range(2 * CG)]
        slice_used = sem("slice_used")
        x_ready = sem("x_ready")
        sum_copied = sem("sum_copied")
        node_put = sem("node_put")
        node_free = sem("node_free")
        x1t_put = sem("x1t_put")
        x1t_copied = sem("x1t_copied")
        sq_in = sem("sq_in")
        sq_out = sem("sq_out")
        var_in = sem("var_in")
        sd_out = sem("sd_out")
        feats_ready = sem("feats_ready")
        ft_put = sem("ft_put")
        ft_copied = sem("ft_copied")
        fc_put = sem("fc_put")
        out_ready = sem("out_ready")
        out_stored = sem("out_stored")
        sp_passed = sem("sp_passed")
        pe_passed = sem("pe_passed")
        pool_passed = sem("pool_passed")
        dve_passed = sem("dve_passed")

        EDGE_ARRAYS = [(gid_f, e_gid), (lo_f, e_all[:, :, 0]), (key_f, e_all[:, :, 1]), (w_f, e_all[:, :, 2]), (dst_f, e_dst)]
        FLAT = "p a b -> p (a b)"

        def edges_view(dram):
            a = FULL_G * P * P
            b = a + REST_T * P
            return (dram[0:a].rearrange("(h p e) -> p h e", p=P, e=P),
                    dram[a:b].rearrange("(p e) -> p e", e=P),
                    dram[b:E].rearrange("(p e) -> p e", p=1))

        PRODUCTS = [(counts_t, x1), (weights_t, x2), (weights_t, x3), (weights_t, u1), (weights_t, u2), (weights_t, u3)]

        def general_tile(eng, lo, done, trip, size, width):
            return nc.s_assert_within(eng.snap(lo + done + trip * size), 0, TP - width, skip_runtime_bounds_check_because=
                                      "the trips end within one trip of the last real tile, which leaves room up to TP")

        def range_of(eng, table, n, most):
            return eng.value_load(table[0:1, bass.ds(n, 1)], min_val=0, max_val=most)

        block = ctx.enter_context(nc.Block())

        @block.sync
        def _(sp):
            sp.dma_start(x0[:, 0:CH - 1, :], x_in[0:(CH - 1) * P, :].rearrange("(c p) f -> p c f", p=P)).then_inc(x_loaded, 16)
            sp.wait_ge(x_tail_zero, 1)
            sp.dma_start(x0[0:LAST, CH - 1, :], x_in[(CH - 1) * P:N, :]).then_inc(x_loaded, 16)
            sp.dma_start(rel_sb[:, :, :], rel_w.rearrange("r i o -> i r o")).then_inc(rel_loaded, 16)
            for n, (dram, tile) in enumerate([(src_in, src_i), (dst_in, dst_i), (type_in, typ_i), (weight_in, w_f)]):
                whole, tiles, rest = edges_view(dram)
                sp.dma_start(tile[:, 0:FULL_G, :], whole).then_inc(main_loaded[n], 16)
                if n == 0:
                    sp.wait_ge(pads_set, 4)
                sp.dma_start(tile[0:REST_T, FULL_G, :], tiles).then_inc(main_loaded[n], 16)
                sp.dma_start(tile[REST_T:REST_T + 1, FULL_G, 0:REST_E], rest).then_inc(main_loaded[n], 16)
            sp.dma_start(l1_rows[:, 0, :], l1_w[:, 0:F]).then_inc(w_loaded, 16)
            sp.dma_start(l1_rows[:, 1, :], l1_w[:, 0:F]).then_inc(w_loaded, 16)
            sp.dma_start(l1_rows[:, 2, :], l1_w[:, F:2 * F]).then_inc(w_loaded, 16)
            sp.dma_start(fc_rows[:, :], fc_w).then_inc(w_loaded, 16)
            sp.dma_start(small_row[0:1, 0:F], l1_b.rearrange("(a n) -> a n", a=1)).then_inc(w_loaded, 16)
            sp.dma_start(small_row[0:1, F:2 * F], fc_b.rearrange("(a n) -> a n", a=1)).then_inc(w_loaded, 16)
            sp.dma_start(small_row[0:1, 2 * F:2 * F + 1], prelu_a.rearrange("(a n) -> a n", a=1)).then_inc(w_loaded, 16)
            sp.wait_ge(range_turned, 1)
            sp.dma_start(range_dram, range_t[:, :]).then_inc(range_stored, 16)
            sp.wait_ge(range_stored, 16)
            sp.dma_start(r_red[:, :, :], range_dram.rearrange("(o m b) p -> o m (b p)", o=1, m=2)).then_inc(range_back, 16)
            sp.sem_inc(blk_free, 2)
            views = [m[0].rearrange("g a p (b s) -> g b p a s", b=GB) for m in (weights_t, counts_t)]
            last_views = [m[1].rearrange("a p (b s) -> b p a s", b=LASTB) for m in (weights_t, counts_t)]

            def store(step, to):
                sp.wait_ge(win_out, WPS * step + WPS + 2)
                sp.sem_inc(sp_passed, 1)
                sp.wait_ge(step_done, step + 1)
                sp.sem_inc(sp_passed, 1)
                for m in range(2):
                    sp.dma_start(to[m], stage[:, bass.ds(step % 2, 1), m, :, :].rearrange("p o (a c) d -> p (o a) (c d)", a=CG)).then_inc(blk_stored, 16)
                sp.wait_ge(blk_stored, 32 * step + 32)
                sp.sem_inc(blk_free, 1)

            with sp.Fori(0, GROUPS - 1) as g:
                for b in range(GB):
                    store(g * GB + b, [view[g, b] for view in views])
            for b in range(LASTB):
                store((GROUPS - 1) * GB + b, [view[b] for view in last_views])

            def load(group, slice_, cg, n, blocks):
                sp.wait_ge(slice_used, CG * group + cg + 1)
                sp.dma_start(ring[:, n * CG + cg, 0:blocks * SL], slice_).then_inc(landed[n * CG + cg], 16)

            for k, (m, _) in enumerate(PRODUCTS):
                with sp.Fori(0, (GROUPS - 1) // 2) as it:
                    for j in range(2):
                        for cg in range(CG):
                            load(GROUPS * k + j + 2 * it, m[0][2 * it + j, cg], cg, (GROUPS * k + j) % 2, GB)
                for cg in range(CG):
                    load(GROUPS * k + GROUPS - 1, m[1][cg], cg, (GROUPS * k + GROUPS - 1) % 2, LASTB)
            sp.wait_ge(out_ready, 1)
            sp.dma_start(out[0:(CH - 1) * P, :].rearrange("(c p) f -> p c f", p=P), ln_h[:, 0:CH - 1, :]).then_inc(out_stored, 16)
            sp.dma_start(out[(CH - 1) * P:N, :], ln_h[0:LAST, CH - 1, :]).then_inc(out_stored, 16)
            sp.wait_ge(out_stored, 32)

        @block.gpsimd
        def _(pool):
            pool.memset(x0[:, CH - 1, :], 0.0).then_inc(x_tail_zero, 1)
            pool.memset(ident[:, :], 0.0).then_inc(consts_step, 1)
            pool.memset(ident2[:, :], 0.0).then_inc(consts_step, 1)
            pool.wait_ge(consts_step, 2)
            pool.affine_select(out=ident[:, :], in_=ident[:, :], compare_op=ALU.not_equal, fill=1.0, base=0,
                               pattern=[[-1, P]], channel_multiplier=1).then_inc(consts_made, 1)
            pool.affine_select(out=ident2[:, :], in_=ident2[:, :], compare_op=ALU.not_equal, fill=1.0, base=0,
                               pattern=[[-1, F]], channel_multiplier=1).then_inc(consts_step, 1)
            pool.wait_ge(consts_step, 3)
            pool.affine_select(out=ident2[:, :], in_=ident2[:, :], compare_op=ALU.not_equal, fill=1.0, base=-F,
                               pattern=[[-1, F]], channel_multiplier=1).then_inc(consts_made, 1)
            ok = dict(allow_small_or_imprecise_dtypes=True)
            for out_, pattern, base, mul in (
                    (iota_b[:, :], [[1, 256]], 0, 0), (iota_f[:, :], [[1, P]], 0, 0), (win_base[:, :], [[WC, WINS]], 0, 0),
                    (first_dst[:, 0:WINS], [[WIN, WINS]], 0, 0), (last_dst[:, 0:WINS], [[WIN, WINS]], WIN - 1, 0),
                    (first_dst[:, WINS:RC], [[P, RC - WINS]], 0, 0), (last_dst[:, WINS:RC], [[P, RC - WINS]], P - 1, 0),
                    (chunk_base[:, :], [[P, STEPS]], 0, 0), (tile_no[:, :], [[P, TG]], 1, 1), (tile_left[:, :], [[-P, TG]], TP, -1)):
                pool.iota(out_, pattern, base=base, channel_multiplier=mul, **ok).then_inc(consts_made, 1)
            pool.memset(x_gathered[:, :, :], 1.0).then_inc(consts_step, 1)
            pool.memset(gathered[:, :, :], 1.0).then_inc(consts_step, 1)
            pool.memset(acc2[:, :, :], 0.0).then_inc(consts_made, 1)
            pool.memset(ones_row[:, :], 1.0).then_inc(consts_made, 1)
            pool.wait_ge(consts_step, 5)
            pool.wait_ge(tables_ready, 1)
            for b in range(YB):
                pool.wait_ge(y_stored[b], 16 * ((CH + YB - 1 - b) // YB))
            with pool.Fori(0, STEPS) as i:
                lo = range_of(pool, tab_lo, WINS + i, TP - TPC)
                for g in range(TPC // GG):
                    pool.wait_ge(rel_done, TPC * i + GG * g + GG)
                    pool.tensor_copy(gid_stage[:, GG * g:GG * g + GG], e_gid[:, bass.ds(lo + GG * g, GG)]).then_inc(ids_staged, 1)
                    pool.wait_ge(ids_staged, TPC // GG * i + g + 1)
                    pool.sem_inc(pool_passed, 1)
                    for s in range(GG * g, GG * g + GG):
                        pool.indirect_dma_start(
                            out=gathered[:, s, 0:F], out_offset=None, in_=y_dram[:, :],
                            in_offset=bass.IndirectOffsetOnAxis(ap=gid_stage[:, s:s + 1], axis=0)).then_inc(row_landed[s], 16)
                ex = range_of(pool, tab_ex, WINS + i, TP // XC)
                with pool.If(ex > 0):
                    cum = range_of(pool, tab_cum, WINS + i, STEPS * TP // XC)
                    with pool.Fori(0, ex) as trip:
                        pool.wait_ge(xd_done, cum + trip + 1)
                        pool.tensor_copy(x_gid_stage[:, :], e_gid[:, bass.ds(general_tile(pool, lo, TPC, trip, XC, XC), XC)]).then_inc(x_ids_staged, 1)
                        pool.wait_ge(x_ids_staged, cum + trip + 1)
                        pool.sem_inc(pool_passed, 1)
                        for q in range(XC):
                            pool.indirect_dma_start(
                                out=x_gathered[:, q, 0:F], out_offset=None, in_=y_dram[:, :],
                                in_offset=bass.IndirectOffsetOnAxis(ap=x_gid_stage[:, q:q + 1], axis=0)).then_inc(x_row_landed[q], 16)

        @block.scalar
        def _(act):
            for q in range(-(-CH // 4)):
                n = min(4, CH - 4 * q) * P
                act.wait_ge(xt_put, q + 1)
                act.copy(xt[:, 512 * q:512 * q + n], ps[0:F, 4 + q % 2, 0:n]).then_inc(xt_copied, 1)
            u = 0
            for _, e_arr in EDGE_ARRAYS:
                for h in range(0, TG, 4):
                    n = min(4, TG - h) * P
                    act.wait_ge(edges_put, u + 1)
                    act.copy(e_arr[:, P * h:P * h + n], ps[:, 4 + u % 2, 0:n]).then_inc(edges_copied, 1)
                    u += 1
            for c in range(CH):
                act.wait_ge(y_put, c + 1)
                if c >= YB:
                    act.wait_ge(y_stored[c % YB], 16 * (c // YB))
                act.copy(y_rows[:, c % YB, :].rearrange("p (b n) -> p b n", b=2), ps[:, 2 * (c % 2):2 * (c % 2) + 2, :]).then_inc(y_copied, 1)
                act.wait_ge(y_copied, c + 1)
                act.dma_start(y_dram.rearrange("(c p r) f -> c p (r f)", p=P, r=RELS)[c], y_rows[:, c % YB, :]).then_inc(y_stored[c % YB], 16)
            act.wait_ge(tables_ready, 1)
            act.sem_inc(win_out, 2)
            act.sem_inc(keyw_ready, 1)

            def stage_window(n, slot):
                lo = range_of(act, tab_lo, n, TP - TPC)
                act.copy(e_stage[:, slot, :].rearrange("p (t k) -> p t k", k=3), e_all[:, bass.ds(lo, TPW), :]).then_inc(staged, 1)

            def put_out(n, j, turn):
                act.wait_ge(win_done, n + 3)
                for m in range(2):
                    last = act.copy(stage[:, bass.ds(turn, 1), m, :, j * WIN:(j + 1) * WIN].rearrange("p o c d -> p (o c) d"),
                                    ps[:, 2 * SLOT[j] + m, 0:WC].rearrange("p (d c) -> p c d", c=CH))
                last.then_inc(win_out, 1)

            for n in range(WPS - 1):
                stage_window(n, n)
            with act.Fori(0, STEPS) as i:
                turn = act.snap(i % 2)
                for j in range(WPS):
                    n = WPS * i + j
                    act.wait_ge(sel_ready, n + 1)
                    for s in range(TPW):
                        last = act.activation(key_w[:, SLOT[j], s, :], key_b[:, SLOT[j], s, 0:WC], ACT.Copy, scale=e_stage[:, j, 3 * s + 2:3 * s + 3])
                    last.then_inc(keyw_ready, 1)
                    act.wait_ge(keyw_ready, n + 1)
                    stage_window(n + WPS - 1, j - 1 if j else WPS - 1)
                    if j == 1:
                        act.wait_ge(blk_free, i + 1)
                    if j:
                        put_out(n - 1, j - 1, turn)
                put_out(WPS * i + WPS - 1, WPS - 1, turn)

            def sums(k):
                for_group = lambda gg, g, n, width: (
                    act.wait_ge(slice_used, CG * (gg + 1) + 2 * CG),
                    act.copy(y_t[:, bass.ds(g * GN, width)], ps[:, n, 0:width]).then_inc(sum_copied, 1))
                if k:
                    act.wait_ge(node_put, k)
                with act.Fori(0, (GROUPS - 1) // 2) as it:
                    for j in range(2):
                        for_group(GROUPS * k + j + 2 * it, 2 * it + j, (GROUPS * k + j) % 2, GN)
                g = GROUPS - 1
                act.wait_ge(slice_used, CG * (GROUPS * k + g + 1) + 2 * CG)
                act.copy(y_t[:, g * GN:g * GN + LASTB * BLK], ps[:, (GROUPS * k + g) % 2, 0:LASTB * BLK]).then_inc(sum_copied, 1)

            def norm(n):
                act.wait_ge(sq_in, n + 1)
                act.activation(ln_q[:, :, :], ln_c[:, :, :], ACT.Square).then_inc(sq_out, 1)
                act.wait_ge(var_in, n + 1)
                act.activation(ln_d[:, n, :], ln_v[:, n, :], ACT.Sqrt).then_inc(sd_out, 1)

            norm(0)
            act.wait_ge(x_ready, 1)
            act.sem_inc(sum_copied, 2)

            for q in range(-(-CH // 4)):
                n = min(4, CH - 4 * q) * P
                act.wait_ge(x1t_put, q + 1)
                act.copy(x1t[:, 512 * q:512 * q + n], ps[0:F, 4 + q % 2, 0:n]).then_inc(x1t_copied, 1)
            sums(0)
            norm(1)
            sums(1)
            norm(2)
            for k in range(2, 6):
                sums(k)
            for j in range(3):
                for q in range(-(-CH // 4)):
                    n = min(4, CH - 4 * q) * P
                    u = 7 * j + q
                    act.wait_ge(ft_put, u + 1)
                    if u >= 2:
                        act.wait_ge(fc_put, u - 1)
                    act.copy(feats_t[:, u % 2, 0:n], ps[:, 4 + u % 2, 0:n]).then_inc(ft_copied, 1)
            norm(3)

        @block.vector
        def _(v):
            steps = [0]

            def link(ins):
                steps[0] += 1
                ins.then_inc(dve_step, 1)
                v.wait_ge(dve_step, steps[0])

            v.memset(dst_i[:, FULL_G, :], -1).then_inc(pads_set, 1)
            v.memset(src_i[:, FULL_G, :], 0).then_inc(pads_set, 1)
            v.memset(typ_i[:, FULL_G, :], 0).then_inc(pads_set, 1)
            v.memset(w_f[:, FULL_G, :], 0.0).then_inc(pads_set, 1)
            v.wait_ge(consts_made, 14)
            for n in range(4):
                v.wait_ge(main_loaded[n], 48)
            v.tensor_copy(scr_f[:, :, :], src_i[:, :, :])
            v.tensor_copy(scr2_f[:, :, :], typ_i[:, :, :])
            link(v.tensor_copy(dst_f[:, :, :], dst_i[:, :, :]))
            v.scalar_tensor_tensor(out=gid_f[:, :, :], in0=scr_f[:, :, :], scalar=float(RELS), in1=scr2_f[:, :, :], op0=ALU.mult, op1=ALU.add)
            v.tensor_scalar(tmp_i[:, :, :], src_i[:, :, :], P - 1, None, ALU.bitwise_and)
            link(v.tensor_scalar(hi_i[:, :, :], src_i[:, :, :], 7, None, ALU.arith_shift_right))
            v.tensor_copy(lo_f[:, :, :], tmp_i[:, :, :])
            link(v.tensor_copy(scr_f[:, :, :], hi_i[:, :, :]))
            v.scalar_tensor_tensor(out=key_f[:, :, :], in0=dst_f[:, :, :], scalar=float(CH), in1=scr_f[:, :, :], op0=ALU.mult, op1=ALU.add).then_inc(edges_ready, 1)
            v.tensor_reduce(t_max[:, :], dst_f[:, :, :], axis=AX.X, op=ALU.max)
            link(v.tensor_scalar(scr2_f[:, :, :], dst_f[:, :, :], 0.0, 5000.0, ALU.is_lt, ALU.mult))
            link(v.tensor_tensor(scr_f[:, :, :], scr2_f[:, :, :], dst_f[:, :, :], ALU.add))
            v.tensor_reduce(t_min[:, :], scr_f[:, :, :], axis=AX.X, op=ALU.min)
            v.memset(r_zero[:, :], 0.0)
            link(v.memset(best[:, :, 0, :], 0.0))
            for h in range(TG):
                last = v.tensor_scalar(has_a[:, h, :], last_dst[:, :], t_min[:, h:h + 1], None, ALU.is_ge)
            link(last)
            for h in range(TG):
                last = v.scalar_tensor_tensor(out=has[:, h, :], in0=first_dst[:, :], scalar=t_max[:, h:h + 1], in1=has_a[:, h, :], op0=ALU.is_le, op1=ALU.mult)
            link(last)
            for h in range(TG):
                a, b = h % 2, (h + 1) % 2
                v.scalar_tensor_tensor(out=best[:, 0, b, :], in0=has[:, h, :], scalar=tile_left[:, h:h + 1], in1=best[:, 0, a, :], op0=ALU.mult, op1=ALU.max)
                link(v.scalar_tensor_tensor(out=best[:, 1, b, :], in0=has[:, h, :], scalar=tile_no[:, h:h + 1], in1=best[:, 1, a, :], op0=ALU.mult, op1=ALU.max))
            v.sem_inc(best_ready, 1)
            v.wait_ge(small_put, 1)
            v.tensor_copy(wa2_t[:, :], ps[:, 6, 0:F])
            v.tensor_copy(wb_t[:, :], ps[0:F, 6, F:2 * F])
            v.tensor_copy(fc_t[:, :, :], ps[:, 6, 128:128 + 3 * F].rearrange("p (j f) -> p j f", f=F))
            v.tensor_copy(small[:, :], ps[:, 6, 352:352 + 2 * F + 1]).then_inc(small_copied, 1)
            v.wait_ge(best_put, 1)
            v.tensor_reduce(range_red[:, :, :], ps[:, 6:8, 0:RC].rearrange("p m (b t) -> p m b t", t=P), axis=AX.X, op=ALU.max).then_inc(range_ready, 1)
            v.wait_ge(range_put, 1)
            v.tensor_copy(range_t[:, :], ps[0:6, 6, 0:P]).then_inc(range_turned, 1)
            v.wait_ge(range_back, 16)
            link(v.tensor_scalar(r_a[:, :], r_red[:, 0, :], -1.0, float(TP), ALU.mult, ALU.add))
            link(v.tensor_scalar(r_lo[:, :], r_a[:, :], float(TP - TPC), None, ALU.min))
            v.tensor_copy(tab_lo[:, :], r_lo[:, :])
            link(v.tensor_tensor(r_k[:, :], r_red[:, 1, :], r_lo[:, :], ALU.subtract))
            for a, b, done, trip in ((0, WINS, TPW, XT), (WINS, RC, TPC, XC)):
                link(v.tensor_scalar(r_a[:, a:b], r_k[:, a:b], -float(done), 0.0, ALU.add, ALU.max))
                link(v.tensor_scalar(r_k[:, a:b], r_a[:, a:b], float(trip - 1), None, ALU.add))
                link(v.tensor_copy(r_ki[:, a:b], r_k[:, a:b]))
                link(v.tensor_scalar(tab_ex[:, a:b], r_ki[:, a:b], trip.bit_length() - 1, None, ALU.arith_shift_right))
                link(v.tensor_copy(r_ex[:, a:b], tab_ex[:, a:b]))
                link(v.tensor_tensor_scan(r_cum[:, a:b], r_ex[:, a:b], r_zero[:, a:b], 0.0, ALU.add, ALU.add))
                link(v.tensor_tensor(r_a[:, a:b], r_cum[:, a:b], r_ex[:, a:b], ALU.subtract))
            v.tensor_copy(tab_cum[:, :], r_a[:, :])
            v.tensor_reduce(tab_any[:, :], r_ex[:, 0:WINS].rearrange("o (i j) -> o i j", j=WPS), axis=AX.X, op=ALU.max).then_inc(tables_ready, 1)
            v.wait_ge(tables_ready, 1)

            v.sem_inc(dsel_ready, DB)
            for b in range(YB):
                v.wait_ge(y_stored[b], 16 * ((CH + YB - 1 - b) // YB))

            def window_slow(i, j, turn):
                n = v.snap(WPS * i + j)
                ex = range_of(v, tab_ex, n, TP // XT)
                with v.If(ex > 0):
                    cum = range_of(v, tab_cum, n, WINS * TP // XT)
                    lo = range_of(v, tab_lo, n, TP - TPC)
                    with v.Fori(0, ex) as trip:
                        t = general_tile(v, lo, TPW, trip, XT, XT)
                        for q in range(XT):
                            v.tensor_scalar(x_key_b[:, q, :], iota_b[:, 0:WS], win_base[:, bass.ds(n, 1)], e_all[:, bass.ds(t + q, 1), 1], ALU.add, ALU.is_equal)
                            v.tensor_scalar(x_sel_b[:, q, :], iota_b[:, 0:P], e_all[:, bass.ds(t + q, 1), 0], None, ALU.is_equal)
                            last = v.tensor_scalar(x_sel_f[:, q, :], iota_f[:, :], e_all[:, bass.ds(t + q, 1), 0], None, ALU.is_equal)
                        last.then_inc(xb_ready, 1)
                        v.wait_ge(xb_ready, cum + trip + 1)
                        for q in range(XT):
                            last = v.tensor_scalar(x_key_w[:, q, :], x_key_b[:, q, :], e_all[:, bass.ds(t + q, 1), 2], None, ALU.mult)
                        last.then_inc(xs_ready, 1)
                        v.wait_ge(x_done, cum + trip + 1)
                        for m in range(2):
                            a = stage[:, bass.ds(turn, 1), m, :, bass.ds(WIN * j, WIN)].rearrange("p o c d -> p (o c) d")
                            last = v.tensor_tensor(a, a, ps[:, 7, WS * m:WS * m + WC].rearrange("p (d c) -> p c d", c=CH), ALU.add)
                        last.then_inc(x_added, 1)
                        v.wait_ge(x_added, cum + trip + 1)
                        v.sem_inc(dve_passed, 1)
                v.sem_inc(dve_passed, 1)

            with v.Fori(0, STEPS) as i:
                lo = range_of(v, tab_lo, WINS + i, TP - TPC)
                v.wait_ge(dsel_ready, DB * i + DB)
                v.tensor_scalar(dst_stage[:, :], e_dst[:, bass.ds(lo, TPC)], chunk_base[:, bass.ds(i, 1)], None, ALU.subtract).then_inc(dst_staged, 1)
                for j in range(WPS):
                    n = WPS * i + j
                    base = win_base[:, bass.ds(n, 1)]
                    v.wait_ge(staged, n + 1)
                    v.wait_ge(win_done, n + 1)
                    v.tensor_tensor(sel_f[:, SLOT[j], :, :], iota_f[:, :].unsqueeze(1).to_broadcast([P, TPW, P]),
                                    e_stage[:, j, 0:3 * TPW:3].unsqueeze(2).to_broadcast([P, TPW, P]), ALU.is_equal).then_inc(self_ready, 1)
                    for s in range(TPW):
                        last = v.tensor_scalar(key_b[:, SLOT[j], s, :], iota_b[:, 0:WS], base, e_stage[:, j, 3 * s + 1:3 * s + 2], ALU.add, ALU.is_equal)
                    last.then_inc(sel_ready, 1)
                    v.wait_ge(self_ready, n + 1)
                    v.tensor_copy(sel_b[:, SLOT[j], :, :], sel_f[:, SLOT[j], :, :]).then_inc(selb_ready, 1)
                    if j == 1:
                        v.wait_ge(rel_done, TPC * i + TPC)
                        v.tensor_copy(acc[:, bass.ds(i, 1), :].rearrange(FLAT), ps[:, 6, 0:D1]).then_inc(rel_out, 1)
                        v.wait_ge(dst_staged, i + 1)
                    if AFTER[j]:
                        a, b = AFTER[j][0], AFTER[j][-1] + 1
                        v.wait_ge(rel_done, TPC * i + b)
                        v.tensor_tensor(dsel[:, a:b, :], iota_f[:, :].unsqueeze(1).to_broadcast([P, b - a, P]),
                                        dst_stage[:, a:b].unsqueeze(2).to_broadcast([P, b - a, P]), ALU.is_equal).then_inc(dsel_ready, 1)
                some = range_of(v, tab_any, i, TP // XT)
                with v.If(some > 0):
                    v.wait_ge(win_out, WPS * i + WPS + 2)
                    v.sem_inc(dve_passed, 1)
                    turn = v.snap(i % 2)
                    with v.Fori(0, WPS) as j:
                        window_slow(i, j, turn)
                v.sem_inc(step_done, 1)
                ex = range_of(v, tab_ex, WINS + i, TP // XC)
                with v.If(ex > 0):
                    cum = range_of(v, tab_cum, WINS + i, STEPS * TP // XC)
                    with v.Fori(0, ex) as trip:
                        t = general_tile(v, lo, TPC, trip, XC, XC)
                        for q in range(XC):
                            last = v.tensor_scalar(x_dsel[:, q, :], iota_f[:, :], chunk_base[:, bass.ds(i, 1)], e_dst[:, bass.ds(t + q, 1)], ALU.add, ALU.is_equal)
                        last.then_inc(xd_ready, 1)
                        v.wait_ge(xd_done, cum + trip + 2)
                        a = acc2[:, bass.ds(i, 1), :].rearrange(FLAT)
                        v.tensor_tensor(a, a, ps[:, 7, 0:D1], ALU.add).then_inc(xd_added, 1)
                        v.wait_ge(xd_added, cum + trip + 1)
                        v.sem_inc(dve_passed, 1)
                v.sem_inc(dve_passed, 1)
            v.wait_ge(rel_done, TPC * STEPS + TPC)
            link(v.tensor_copy(acc[:, STEPS, :], ps[:, 6, 0:D1]))
            v.wait_ge(win_out, WINS + 2)
            v.wait_ge(win_done, WINS + 2)
            v.wait_ge(blk_free, STEPS + 2)

            def bcast(m):
                return m.unsqueeze(2).to_broadcast([P, CH, F])

            def norm(n, x_out):
                link(v.tensor_reduce(ln_s[:, n, :], ln_h[:, :, :], axis=AX.X, op=ALU.add))
                link(v.tensor_scalar(ln_m[:, n, :], ln_s[:, n, :], 1.0 / F, None, ALU.mult))
                if n:
                    v.wait_ge(sq_out, n)
                v.tensor_tensor(ln_c[:, :, :], ln_h[:, :, :], bcast(ln_m[:, n, :]), ALU.subtract).then_inc(sq_in, 1)
                v.wait_ge(sq_out, n + 1)
                link(v.tensor_reduce(ln_s[:, n, :], ln_q[:, :, :], axis=AX.X, op=ALU.add))
                v.tensor_scalar(ln_v[:, n, :], ln_s[:, n, :], 1.0 / F, EPS, ALU.mult, ALU.add).then_inc(var_in, 1)
                v.wait_ge(sd_out, n + 1)
                link(v.reciprocal(ln_r[:, n, :], ln_d[:, n, :]))
                return v.tensor_tensor(x_out[:, :, :], ln_c[:, :, :], bcast(ln_r[:, n, :]), ALU.mult)

            node_sums = ps[:, 2:6, :].rearrange("p b n -> p (b n)")[:, 0:CH * F].rearrange("p (c f) -> p c f", f=F)
            link(v.tensor_tensor(acc[:, 1:1 + CH, :], acc[:, 1:1 + CH, :], acc2[:, :, :], ALU.add))
            v.tensor_scalar(deg[:, :], acc[:, 1:1 + CH, F], 1.0, None, ALU.max)
            link(v.tensor_tensor(ln_h[:, :, :], x0[:, :, :], acc[:, 1:1 + CH, 0:F], ALU.add))
            v.reciprocal(rdeg[:, :], deg[:, :])
            norm(0, x1).then_inc(x_ready, 1)
            v.wait_ge(node_put, 1)
            v.wait_ge(x_ready, 1)
            link(v.tensor_tensor(ln_h[:, :, :], node_sums, bcast(rdeg[:, :]), ALU.mult))
            own = [ps[:, b, :].rearrange("p (c f) -> p c f", f=F) for b in (6, 7, 0, 1)]
            for i, b in enumerate(own):
                n = min(8, CH - 8 * i)
                last = v.tensor_tensor(ln_c[:, 8 * i:8 * i + n, :], b[:, 0:n, :], x1[:, 8 * i:8 * i + n, :], ALU.add)
            link(last)
            v.tensor_tensor(ln_q[:, :, :], ln_c[:, :, :], small[:, 0:F].unsqueeze(1).to_broadcast([P, CH, F]), ALU.add).then_inc(node_free, 1)
            v.wait_ge(node_free, 1)
            link(v.tensor_tensor(ln_h[:, :, :], ln_h[:, :, :], ln_q[:, :, :], ALU.add))
            norm(1, x2).then_inc(x_ready, 1)
            v.wait_ge(node_put, 2)
            v.wait_ge(x_ready, 2)
            v.tensor_tensor(ln_h[:, :, :], node_sums, x2[:, :, :], ALU.add).then_inc(node_free, 1)
            v.wait_ge(node_free, 2)
            norm(2, x3).then_inc(x_ready, 1)
            u4 = ln_h
            for k, u in ((2, u1), (3, u2), (4, u3), (5, u4)):
                v.wait_ge(node_put, k + 1)
                if k == 2:
                    v.wait_ge(x_ready, 3)
                v.tensor_copy(u[:, :, :], node_sums).then_inc(x_ready, 1)
            v.wait_ge(x_ready, 7)
            pairs = [(None, (u1, u2)), ((u2, u4), (u2, u1)), ((u3, u2), (u4, u3))]
            for j, pair in enumerate(pairs):
                if j:
                    v.wait_ge(ft_put, 7 * j)
                for i, ab in enumerate(pair):
                    if ab is None:
                        last = v.tensor_copy(feats[:, :, i, :], u4[:, :, :])
                    else:
                        tmp = (ln_c, ln_q)[i]
                        link(v.tensor_tensor(tmp[:, :, :], ab[0][:, :, :], ab[1][:, :, :], ALU.subtract))
                        last = v.scalar_tensor_tensor(out=feats[:, :, i, :], in0=tmp[:, :, :], scalar=-1.0, in1=tmp[:, :, :], op0=ALU.mult, op1=ALU.max)
                last.then_inc(feats_ready, 1)
            v.wait_ge(fc_put, 21)
            v.wait_ge(feats_ready, 3)
            fc_sums = [ps[:, b, :].rearrange("p (c f) -> p c f", f=F) for b in (0, 1, 2, 3)]
            for i, b in enumerate(fc_sums):
                n = min(8, CH - 8 * i)
                last = v.tensor_tensor(ln_c[:, 8 * i:8 * i + n, :], b[:, 0:n, :], small[:, F:2 * F].unsqueeze(1).to_broadcast([P, n, F]), ALU.add)
            link(last)
            v.tensor_scalar(feats[:, :, 0, :], ln_c[:, :, :], 0.0, small[:, 2 * F:2 * F + 1], ALU.min, ALU.mult)
            link(v.scalar_tensor_tensor(out=ln_q[:, :, :], in0=ln_c[:, :, :], scalar=0.0, in1=x3[:, :, :], op0=ALU.max, op1=ALU.add))
            link(v.tensor_tensor(ln_h[:, :, :], ln_q[:, :, :], feats[:, :, 0, :], ALU.add))
            link(norm(3, x1))
            v.tensor_copy(ln_h[:, :, :], x1[:, :, :]).then_inc(out_ready, 1)

        @block.tensor
        def _(pe):
            def transposed(x, put, copied, wait_first):
                for q in range(-(-CH // 4)):
                    if q >= 2:
                        pe.wait_ge(copied, q - 1)
                    for c in range(4 * q, min(4 * q + 4, CH)):
                        last = pe.transpose(ps[0:F, 4 + q % 2, P * (c % 4):P * (c % 4) + P], x[:, c, :], ident[:, :])
                    last.then_inc(put, 1)

            pe.wait_ge(consts_made, 14)
            pe.wait_ge(x_loaded, 32)
            transposed(x0, xt_put, xt_copied, None)
            pe.wait_ge(edges_ready, 1)
            u = 0
            for f_arr, _ in EDGE_ARRAYS:
                for h in range(0, TG, 4):
                    if u >= 2:
                        pe.wait_ge(edges_copied, u - 1)
                    elif u == 0:
                        pe.wait_ge(xt_copied, -(-CH // 4))
                    for g in range(h, min(h + 4, TG)):
                        last = pe.transpose(ps[:, 4 + u % 2, P * (g - h):P * (g - h) + P], f_arr[:, g, :], ident[:, :])
                    last.then_inc(edges_put, 1)
                    u += 1
            pe.wait_ge(w_loaded, 16 * 7)
            pe.transpose(ps[:, 6, 0:F], l1_rows[:, 0:2, :].rearrange(FLAT), ident[0:F, 0:F])
            pe.transpose(ps[0:F, 6, F:2 * F], l1_rows[:, 2, :], ident[0:F, 0:F])
            for j in range(3):
                pe.transpose(ps[:, 6, 128 + F * j:128 + F * j + F], fc_rows[:, P * j:P * j + P], ident[0:F, 0:F])
            pe.matmul(ps[:, 6, 352:352 + 2 * F + 1], ones_row[:, :], small_row[:, :], start=True, stop=True).then_inc(small_put, 1)
            def ranges():
                pe.wait_ge(best_ready, 1)
                pe.wait_ge(small_copied, 1)
                for m in range(2):
                    for b in range(3):
                        last = pe.transpose(ps[:, 6 + m, P * b:P * b + P], best[:, m, TG % 2, P * b:P * b + P], ident[:, :])
                last.then_inc(best_put, 1)
                pe.wait_ge(range_ready, 1)
                pe.transpose(ps[0:6, 6, 0:P], range_red[:, :, :].rearrange(FLAT), ident[:, :]).then_inc(range_put, 1)

            pe.wait_ge(rel_loaded, 16)
            for c in range(CH):
                if c == 8:
                    ranges()
                pe.wait_ge(xt_copied, c // 4 + 1)
                if c >= 2:
                    pe.wait_ge(y_copied, c - 1)
                for i in range(2):
                    last = pe.matmul(ps[:, 2 * (c % 2) + i, :], xt[:, c * P:c * P + P], rel_sb[:, 8 * i:8 * i + 8, :].rearrange("i r o -> i (r o)"), start=True, stop=True)
                last.then_inc(y_put, 1)
            pe.wait_ge(tables_ready, 1)
            pe.sem_inc(win_done, 2)
            pe.sem_inc(rel_done, TPC)
            pe.sem_inc(xd_done, 1)
            with pe.Fori(0, STEPS) as i:
                for j in range(WPS):
                    n = WPS * i + j
                    pe.wait_ge(selb_ready, n + 1)
                    pe.wait_ge(keyw_ready, n + 2)
                    pe.wait_ge(win_out, n + 1)
                    for s in range(TPW):
                        at = dict(start=(s == 0), stop=(s == TPW - 1))
                        pe.matmul(ps[:, 2 * SLOT[j], 0:WC], sel_f[:, SLOT[j], s, :], key_w[:, SLOT[j], s, :], **at)
                        last = pe.matmul(ps[:, 2 * SLOT[j] + 1, 0:WC], sel_b[:, SLOT[j], s, :], key_b[:, SLOT[j], s, 0:WC], **at)
                    last.then_inc(win_done, 1)
                    if AFTER[j]:
                        pe.wait_ge(dsel_ready, DB * i + DB + j - 1)
                    for s in AFTER[j]:
                        pe.wait_ge(row_landed[s], 16 * i + 16)
                        if s == 0:
                            pe.wait_ge(rel_out, i + 1)
                        pe.matmul(ps[:, 6, 0:D1], dsel[:, s, :], gathered[:, s, :], start=(s == 0), stop=(s == TPC - 1)).then_inc(rel_done, 1)
                some = range_of(pe, tab_any, i, TP // XT)
                with pe.If(some > 0):
                    with pe.Fori(0, WPS) as j:
                        n = pe.snap(WPS * i + j)
                        ex = range_of(pe, tab_ex, n, TP // XT)
                        with pe.If(ex > 0):
                            cum = range_of(pe, tab_cum, n, WINS * TP // XT)
                            with pe.Fori(0, ex) as trip:
                                pe.wait_ge(xs_ready, cum + trip + 1)
                                for q in range(XT):
                                    pe.matmul(ps[:, 7, 0:WC], x_sel_f[:, q, :], x_key_w[:, q, 0:WC], start=(q == 0), stop=(q == XT - 1))
                                for q in range(XT):
                                    last = pe.matmul(ps[:, 7, WS:WS + WC], x_sel_b[:, q, :], x_key_b[:, q, 0:WC], start=(q == 0), stop=(q == XT - 1))
                                last.then_inc(x_done, 1)
                        pe.sem_inc(pe_passed, 1)
                ex = range_of(pe, tab_ex, WINS + i, TP // XC)
                with pe.If(ex > 0):
                    cum = range_of(pe, tab_cum, WINS + i, STEPS * TP // XC)
                    with pe.Fori(0, ex) as trip:
                        pe.wait_ge(xd_ready, cum + trip + 1)
                        for q in range(XC):
                            pe.wait_ge(x_row_landed[q], (cum + trip) * 16 + 16)
                            last = pe.matmul(ps[:, 7, 0:D1], x_dsel[:, q, :], x_gathered[:, q, :], start=(q == 0), stop=(q == XC - 1))
                        last.then_inc(xd_done, 1)
                pe.sem_inc(pe_passed, 1)

            pe.wait_ge(x_ready, 1)
            transposed(x1, x1t_put, x1t_copied, None)
            pe.sem_inc(slice_used, 2 * CG)

            def column_group(gg, use, n, x, blocks):
                pe.wait_ge(sum_copied, gg + 1)
                for cg in range(CG):
                    pe.wait_ge(landed[n * CG + cg], use * 16 + 16)
                    m = ring[:, n * CG + cg, :].rearrange("p (b c d) -> p b c d", b=GB, d=BLK)
                    for ci in range(CI):
                        c = cg * CI + ci
                        o = ps[F * (c % 2):F * (c % 2) + F, n, 0:blocks * BLK].rearrange("p (b d) -> p b d", d=BLK)
                        last = pe.matmul(o, x[:, c, :], m[:, 0:blocks, ci, :], start=(c < 2), stop=(c >= CH - 2))
                    last.then_inc(slice_used, 1)

            def product(k, x, rhs, per):
                with pe.Fori(0, (GROUPS - 1) // 2) as it:
                    for j in range(2):
                        gg = GROUPS * k + j
                        column_group(gg + 2 * it, gg // 2 + it, gg % 2, x, GB)
                gg = GROUPS * k + GROUPS - 1
                column_group(gg, gg // 2, gg % 2, x, LASTB)
                pe.wait_ge(sum_copied, GROUPS * (k + 1) + 2)
                for c in range(CH):
                    last = pe.matmul(ps[:, 2 + c // 8, F * (c % 8):F * (c % 8) + F], y_t[:, c * P:c * P + P], rhs, start=True, stop=True)
                return last

            for k, (_, x) in enumerate(PRODUCTS):
                if k:
                    pe.wait_ge(x_ready, k + 1)
                last = product(k, x, wa2_t[:, :] if k == 0 else ident2[:, :], None)
                if k == 0:
                    pe.wait_ge(x1t_copied, -(-CH // 4))
                    for c in range(CH):
                        b = (6, 7, 0, 1)[c // 8]
                        last = pe.matmul(ps[:, b, F * (c % 8):F * (c % 8) + F], x1t[:, c * P:c * P + P], wb_t[:, :], start=True, stop=True)
                last.then_inc(node_put, 1)
                if k == 0:
                    pe.wait_ge(node_free, 1)
            for j in range(3):
                pe.wait_ge(feats_ready, j + 1)
                for q in range(-(-CH // 4)):
                    u = 7 * j + q
                    if u >= 2:
                        pe.wait_ge(ft_copied, u - 1)
                    chunks = range(4 * q, min(4 * q + 4, CH))
                    for c in chunks:
                        last = pe.transpose(ps[:, 4 + u % 2, P * (c % 4):P * (c % 4) + P], feats[:, c, :, :].rearrange(FLAT), ident[:, :])
                    last.then_inc(ft_put, 1)
                    pe.wait_ge(ft_copied, u + 1)
                    for c in chunks:
                        last = pe.matmul(ps[:, c // 8, F * (c % 8):F * (c % 8) + F], feats_t[:, u % 2, P * (c % 4):P * (c % 4) + P], fc_t[:, j, :],
                                         start=(j == 0 and c % 8 == 0), stop=(j == 2), skip_group_check=True)
                    last.then_inc(fc_put, 1)


_INS = [("x", "x"), ("src", "src"), ("dst", "dst"), ("edge_type_16", "type"), ("edge_weight", "weight"),
        ("L0_gnn_weight", "rel_w"), ("L1_gnn_W", "l1_w"), ("L1_gnn_b", "l1_b"), ("L3_gnn_fc_w", "fc_w"),
        ("L3_gnn_bias", "fc_b"), ("L3_gnn_prelu_a", "prelu_a")]


def kernel(**inputs):
    import numpy as np
    import concourse.bacc as bacc
    from concourse import mybir as _mybir
    from concourse.bass_utils import run_bass_kernel_spmd as run

    nc = bacc.Bacc("TRN2", target_bir_lowering=False, num_devices=1)
    arrays, args = {}, []
    for name, short in _INS:
        a = np.ascontiguousarray(inputs[name])
        if a.ndim == 0:
            a = a.reshape(1)
        arrays[short] = a
        args.append(nc.dram_tensor(short, a.shape, _mybir.dt.from_np(a.dtype), kind="ExternalInput").ap())
    out = nc.dram_tensor("out", (N, F), F32, kind="ExternalOutput").ap()
    build(nc, *args, out)
    r = run(nc, [arrays], core_ids=[0])
    return r.results[0]["out"]
```

```python
import concourse.bass as bass
import concourse.mybir as mybir
from contextlib import ExitStack

F32 = mybir.dt.float32
BF16 = mybir.dt.bfloat16
I32 = mybir.dt.int32
ALU = mybir.AluOpType
ACT = mybir.ActivationFunctionType
AX = mybir.AxisListType

P = 128
N = 3125
E = 103125
F = 64
RELS = 16
EPS = 1e-5

CH = -(-N // P)
LAST = N - (CH - 1) * P
TILES = -(-E // P)
TG = -(-TILES // P)
TP = TG * P
FULL_G = E // (P * P)
REST_T = (E - FULL_G * P * P) // P
REST_E = E - (FULL_G * P + REST_T) * P

WIN = 10
WC = WIN * CH
WS = WC + 2
TPW = 4
STEPS = CH
WPS = -(-CH * P // (STEPS * WIN))
WINS = STEPS * WPS
BLK = WPS * WIN
TPC = 35
GG = 7
XT = 8
XC = 8
RC = 3 * P
SLOTS = 4
SLOT = [j % 3 for j in range(WPS - 1)] + [3]
AFTER = [[] for _ in range(2)] + [list(range(TPC * j // (WPS - 2), TPC * (j + 1) // (WPS - 2))) for j in range(WPS - 2)]
DB = WPS - 2
assert TPC % GG == 0 and WPS % 3 == 1 and WINS + STEPS <= RC and TILES + XC + TPC < TP

YB = 4
GB = 3
GROUPS = -(-STEPS // GB)
GN = GB * BLK
LASTB = STEPS - (GROUPS - 1) * GB
COLS = STEPS * BLK
CG = 5
CI = CH // CG
SL = CI * BLK
RES = 3
ORDER = [3, 0, 4, 1, 5, 2, 6, 7, 8]
BANK = [0, 1] * ((GROUPS - 1) // 2) + [6]
STREAMED = [p for p, g in enumerate(ORDER) if g >= RES]
assert GROUPS % 2 == 1 and ORDER[-1] == GROUPS - 1
D1 = F + 1


def build(nc, x_in, src_in, dst_in, type_in, weight_in, rel_w, l1_w, l1_b, fc_w, fc_b, prelu_a, out):
    with ExitStack() as ctx:
        def sb(name, shape, dt=F32):
            return ctx.enter_context(nc.sbuf_tensor(name, shape, dt))

        def sem(name):
            return ctx.enter_context(nc.semaphore(name))

        class Part:

            def __init__(self, whole, start, end):
                self.tensor, self.start, self.at, self.size = whole.tensor, start, start, end

            def restart(self):
                self.at = self.start

            def take(self, shape, dt=F32):
                count = 1
                for n in shape[1:]:
                    count *= n
                words = -(-count * (2 if dt == BF16 else 4) // 4)
                a = self.tensor[0:shape[0], self.at // 4:self.at // 4 + words]
                self.at += 4 * words
                assert self.at <= self.size, (self.at, self.size)
                a = a if dt == F32 else a.bitcast(dt)
                if len(shape) == 3:
                    a = a.rearrange("p (a b) -> p a b", b=shape[2])
                if len(shape) == 4:
                    a = a.rearrange("p (a b c) -> p a b c", b=shape[2], c=shape[3])
                if len(shape) == 5:
                    a = a.rearrange("p (a b c d) -> p a b c d", b=shape[2], c=shape[3], d=shape[4])
                return a

        class Arena(Part):
            def __init__(self, name, size):
                self.start, self.at, self.size = 0, 0, size
                self.tensor = sb(name, [P, size // 4])

        slice_bytes, node_bytes = GB * SL * 4, CH * F * 4
        body = Arena("body", (1 + RES) * CG * slice_bytes + 5 * node_bytes)
        PREP = 74336
        prep, loop = Part(body, 0, PREP), Part(body, PREP, body.size)

        y_dram = nc.dram_tensor("rel_rows", (CH * P * RELS, F), F32, kind="Internal").ap()

        def matrix(name):
            return (nc.dram_tensor(name, (GROUPS - 1, CG, P, GB * SL), F32, kind="Internal").ap(),
                    nc.dram_tensor(name + "_last", (CG, P, LASTB * SL), F32, kind="Internal").ap())

        weights_t, counts_t = matrix("weights_t"), matrix("counts_t")
        range_dram = nc.dram_tensor("ranges", (6, P), F32, kind="Internal").ap()


        ident = sb("ident", [P, P])
        ident2 = sb("ident2", [P, F])
        wa2_t = sb("wa2_t", [P, F])
        wb_t = sb("wb_t", [F, F])
        fc_t = sb("fc_t", [P, 3, F])
        small = sb("small", [P, 2 * F + 1])
        src_i = prep.take([P, TG, P], I32)
        dst_i = prep.take([P, TG, P], I32)
        typ_i = prep.take([P, TG, P], I32)
        tmp_i = prep.take([P, TG, P], I32)
        hi_i = typ_i
        w_f = prep.take([P, TG, P])
        dst_f = prep.take([P, TG, P])
        lo_f = prep.take([P, TG, P])
        key_f = prep.take([P, TG, P])
        gid_f = prep.take([P, TG, P])
        scr_f = prep.take([P, TG, P])
        scr2_f = prep.take([P, TG, P])
        has_a = prep.tensor[:, 0:TG * RC].rearrange("p (a b) -> p a b", b=RC)
        assert RC <= 3 * P
        has = prep.take([P, TG, RC])
        best = prep.take([P, 2, 2, RC])
        tile_no = prep.take([P, TG])
        tile_left = prep.take([P, TG])
        t_min = prep.take([P, TG])
        t_max = prep.take([P, TG])
        first_dst = prep.take([P, RC])
        last_dst = prep.take([P, RC])
        range_red = prep.take([P, 2, 3])
        range_t = prep.take([6, P])
        e_all = loop.take([P, TP, 3])
        e_dst = loop.take([P, TP])
        e_gid = loop.take([P, TP], I32)
        r_red = prep.take([1, 2, RC])
        r_a, r_lo, r_k, r_ex, r_zero, r_cum = [prep.take([1, RC]) for _ in range(6)]
        r_ki = prep.take([1, RC], I32)
        sel_f = loop.take([P, SLOTS, TPW, P])
        sel_b = loop.take([P, SLOTS, TPW, P], BF16)
        key_b = loop.take([P, SLOTS, TPW, WS], BF16)
        key_w = loop.take([P, SLOTS, TPW, WC])
        dst_stage = loop.take([P, TPC])
        dsel = loop.take([P, TPC, P])
        slots_end, loop.at = loop.at, loop.start + 5 * TP * 4
        xt = loop.take([F, CH * P])
        rel_sb = loop.take([F, RELS, F])
        l1_rows = loop.take([F, 3, F])
        fc_rows = loop.take([F, 7 * F])
        small_row = loop.take([1, 2 * F + 1])
        y_rows = loop.take([P, YB, RELS * F])
        loop.at = max(loop.at, slots_end)
        prep.restart()
        stage = prep.take([P, 2, 2, CH, BLK])
        x_sel_f = prep.take([P, XT, P])
        x_sel_b = prep.take([P, XT, P], BF16)
        x_key_b = prep.take([P, XT, WS], BF16)
        x_key_w = prep.take([P, XT, WS])
        x_dsel = prep.take([P, XC, P])
        gathered = loop.take([P, TPC, D1])
        x_gathered = loop.take([P, XC, D1])
        iota_b = loop.take([P, 256], BF16)
        iota_f = loop.take([P, P])
        win_base = loop.take([P, WINS])
        chunk_base = loop.take([P, STEPS])
        ones_row = loop.take([1, P])
        tab_lo = loop.take([1, RC], I32)
        tab_ex = loop.take([1, RC], I32)
        tab_cum = loop.take([1, RC], I32)
        tab_any = loop.take([1, STEPS], I32)
        e_stage = loop.take([P, WPS, TPW * 3])
        gid_stage = loop.take([P, TPC], I32)
        x_gid_stage = loop.take([P, XC], I32)
        acc = loop.take([P, 1 + STEPS, D1])
        acc2 = loop.take([P, 1 + STEPS, D1])
        x0 = sb("x0", [P, CH, F])
        y_t = sb("y_t", [P, COLS])
        body.restart()
        ring = body.take([P, CG, GB * SL])
        resident_start = body.at
        resident = body.take([P, RES * CG, GB * SL])
        cur = body.take([P, CH, F])
        kept = body.take([P, 4, CH, F])
        x3, u1, u2, u3 = [kept[:, k, :, :] for k in range(4)]
        ln_h, x1, ln_c = x0, u1, u3
        body.at = resident_start + CG * slice_bytes
        x1t = body.take([F, CH * P])
        body.at = resident_start
        feats = body.take([P, 2, CH, 2, F])
        feats_t = body.take([P, 2, 512])
        diffs = body.take([P, 2, CH, F])
        fc_out = body.take([P, CH, F])
        fc_neg = body.take([P, CH, F])
        fc_sum = body.take([P, CH, F])
        result = body.take([P, CH, F])
        ln_m = sb("ln_m", [P, 4, CH])
        ln_s = sb("ln_s", [P, 4, CH])
        ln_v = sb("ln_v", [P, 4, CH])
        ln_d = sb("ln_d", [P, 4, CH])
        ln_r = sb("ln_r", [P, 4, CH])
        deg = sb("deg", [P, CH])
        rdeg = sb("rdeg", [P, CH])

        ps = ctx.enter_context(nc.psum_tensor("ps", [P, 8, 512], F32))

        pads_set = sem("pads_set")
        main_loaded = [sem(f"loaded_{n}") for n in ("src", "dst", "typ", "w")]
        x_loaded = sem("x_loaded")
        x_tail_zero = sem("x_tail_zero")
        rel_loaded = sem("rel_loaded")
        w_loaded = sem("w_loaded")
        consts_made = sem("consts_made")
        consts_step = sem("consts_step")
        dve_step = sem("dve_step")
        xt_put = sem("xt_put")
        xt_copied = sem("xt_copied")
        y_put = sem("y_put")
        y_copied = sem("y_copied")
        y_stored = [sem(f"y_stored_{i}") for i in range(YB)]
        fc_step = sem("fc_step")
        small_put = sem("small_put")
        small_copied = sem("small_copied")
        edges_ready = sem("edges_ready")
        edges_put = sem("edges_put")
        edges_copied = sem("edges_copied")
        best_ready = sem("best_ready")
        best_put = sem("best_put")
        range_ready = sem("range_ready")
        range_put = sem("range_put")
        range_turned = sem("range_turned")
        range_stored = sem("range_stored")
        range_back = sem("range_back")
        tables_ready = sem("tables_ready")
        staged = sem("staged")
        self_ready = sem("self_ready")
        sel_ready = sem("sel_ready")
        selb_ready = sem("selb_ready")
        keyw_ready = sem("keyw_ready")
        win_done = sem("win_done")
        win_out = sem("win_out")
        step_done = sem("step_done")
        blk_free = sem("blk_free")
        blk_stored = sem("blk_stored")
        xb_ready = sem("xb_ready")
        xs_ready = sem("xs_ready")
        x_done = sem("x_done")
        x_added = sem("x_added")
        ids_staged = sem("ids_staged")
        row_landed = [sem(f"row_landed_{s}") for s in range(TPC)]
        dst_staged = sem("dst_staged")
        dsel_ready = sem("dsel_ready")
        rel_done = sem("rel_done")
        rel_out = sem("rel_out")
        pe_through = sem("pe_through")
        pool_through = sem("pool_through")
        x_ids_staged = sem("x_ids_staged")
        x_row_landed = [sem(f"x_row_landed_{s}") for s in range(XC)]
        xd_ready = sem("xd_ready")
        xd_done = sem("xd_done")
        xd_added = sem("xd_added")
        landed = [sem(f"slice_landed_{s}") for s in range(CG)]
        resident_landed = [sem(f"resident_landed_{r}") for r in range(RES)]
        slice_used = sem("slice_used")
        x_ready = sem("x_ready")
        sum_copied = sem("sum_copied")
        cur_kept = sem("cur_kept")
        node_put = sem("node_put")
        node_free = sem("node_free")
        x1t_put = sem("x1t_put")
        x1t_copied = sem("x1t_copied")
        deg_ready = sem("deg_ready")
        sq_in = sem("sq_in")
        sq_out = sem("sq_out")
        var_in = sem("var_in")
        sd_out = sem("sd_out")
        diff_ready = sem("diff_ready")
        feats_ready = sem("feats_ready")
        ft_put = sem("ft_put")
        ft_copied = sem("ft_copied")
        fc_put = sem("fc_put")
        out_ready = sem("out_ready")
        out_stored = sem("out_stored")
        sp_passed = sem("sp_passed")
        pe_passed = sem("pe_passed")
        pool_passed = sem("pool_passed")
        dve_passed = sem("dve_passed")

        EDGE_ARRAYS = [(gid_f, e_gid), (lo_f, e_all[:, :, 0]), (key_f, e_all[:, :, 1]), (w_f, e_all[:, :, 2]), (dst_f, e_dst)]
        FLAT = "p a b -> p (a b)"

        def edges_view(dram):
            a = FULL_G * P * P
            b = a + REST_T * P
            return (dram[0:a].rearrange("(h p e) -> p h e", p=P, e=P),
                    dram[a:b].rearrange("(p e) -> p e", e=P),
                    dram[b:E].rearrange("(p e) -> p e", p=1))

        KP = 6

        def general_tile(eng, lo, done, trip, size, width):
            return nc.s_assert_within(eng.snap(lo + done + trip * size), 0, TP - width, skip_runtime_bounds_check_because=
                                      "the trips end within one trip of the last real tile, which leaves room up to TP")

        def range_of(eng, table, n, most):
            return eng.value_load(table[0:1, bass.ds(n, 1)], min_val=0, max_val=most)

        block = ctx.enter_context(nc.Block())

        @block.sync
        def _(sp):
            sp.dma_start(x0[:, 0:CH - 1, :], x_in[0:(CH - 1) * P, :].rearrange("(c p) f -> p c f", p=P)).then_inc(x_loaded, 16)
            sp.wait_ge(x_tail_zero, 1)
            sp.dma_start(x0[0:LAST, CH - 1, :], x_in[(CH - 1) * P:N, :]).then_inc(x_loaded, 16)
            sp.dma_start(rel_sb[:, :, :], rel_w.rearrange("r i o -> i r o")).then_inc(rel_loaded, 16)
            for n, (dram, tile) in enumerate([(src_in, src_i), (dst_in, dst_i), (type_in, typ_i), (weight_in, w_f)]):
                whole, tiles, rest = edges_view(dram)
                sp.dma_start(tile[:, 0:FULL_G, :], whole).then_inc(main_loaded[n], 16)
                if n == 0:
                    sp.wait_ge(pads_set, 4)
                sp.dma_start(tile[0:REST_T, FULL_G, :], tiles).then_inc(main_loaded[n], 16)
                sp.dma_start(tile[REST_T:REST_T + 1, FULL_G, 0:REST_E], rest).then_inc(main_loaded[n], 16)
            sp.dma_start(l1_rows[:, 0, :], l1_w[:, 0:F]).then_inc(w_loaded, 16)
            sp.dma_start(l1_rows[:, 1, :], l1_w[:, 0:F]).then_inc(w_loaded, 16)
            sp.dma_start(l1_rows[:, 2, :], l1_w[:, F:2 * F]).then_inc(w_loaded, 16)
            sp.dma_start(fc_rows[:, 0:F], fc_w[:, 0:F]).then_inc(w_loaded, 16)
            for at, first, n in ((1, 0, 2), (3, 4, 1), (4, 2, 1), (5, 5, 1), (6, 3, 1)):
                sp.dma_start(fc_rows[:, at * F:(at + n) * F], fc_w[:, first * F:(first + n) * F]).then_inc(w_loaded, 16)
            sp.dma_start(small_row[0:1, 0:F], l1_b.rearrange("(a n) -> a n", a=1)).then_inc(w_loaded, 16)
            sp.dma_start(small_row[0:1, F:2 * F], fc_b.rearrange("(a n) -> a n", a=1)).then_inc(w_loaded, 16)
            sp.dma_start(small_row[0:1, 2 * F:2 * F + 1], prelu_a.rearrange("(a n) -> a n", a=1)).then_inc(w_loaded, 16)
            sp.wait_ge(range_turned, 1)
            sp.dma_start(range_dram, range_t[:, :]).then_inc(range_stored, 16)
            sp.wait_ge(range_stored, 16)
            sp.dma_start(r_red[:, :, :], range_dram.rearrange("(o m b) p -> o m (b p)", o=1, m=2)).then_inc(range_back, 16)
            sp.sem_inc(blk_free, 2)
            views = [m[0].rearrange("g a p (b s) -> g b p a s", b=GB) for m in (weights_t, counts_t)]
            last_views = [m[1].rearrange("a p (b s) -> b p a s", b=LASTB) for m in (weights_t, counts_t)]

            def store(step, to):
                sp.wait_ge(win_out, WPS * step + WPS + 3)
                sp.sem_inc(sp_passed, 1)
                sp.wait_ge(step_done, step + 1)
                sp.sem_inc(sp_passed, 1)
                for m in range(2):
                    sp.dma_start(to[m], stage[:, bass.ds(step % 2, 1), m, :, :].rearrange("p o (a c) d -> p (o a) (c d)", a=CG)).then_inc(blk_stored, 16)
                sp.wait_ge(blk_stored, 32 * step + 32)
                sp.sem_inc(blk_free, 1)

            with sp.Fori(0, GROUPS - 1) as g:
                for b in range(GB):
                    store(g * GB + b, [view[g, b] for view in views])
            for b in range(LASTB):
                store((GROUPS - 1) * GB + b, [view[b] for view in last_views])

            def load(m, g, used):
                for cg in range(CG):
                    sp.wait_ge(slice_used, CG * used + cg + 1)
                    if isinstance(g, int) and g == GROUPS - 1:
                        sp.dma_start(ring[:, cg, 0:LASTB * SL], m[1][cg]).then_inc(landed[cg], 16)
                    else:
                        sp.dma_start(ring[:, cg, :], m[0][g, cg]).then_inc(landed[cg], 16)

            with sp.Fori(0, GROUPS - 1) as g:
                load(counts_t, g, g)
            load(counts_t, GROUPS - 1, GROUPS - 1)

            def load_product(k, keep):
                used = GROUPS * k
                for p, g in enumerate(ORDER):
                    if p in STREAMED:
                        load(weights_t, g, used)
                        used = GROUPS * k + p + 1
                    elif keep:
                        if g == 0:
                            sp.wait_ge(node_put, 1)
                        for cg in range(CG):
                            sp.dma_start(resident[:, CG * g + cg, :], weights_t[0][g, cg]).then_inc(resident_landed[g], 16)

            load_product(1, True)
            with sp.Fori(2, KP) as k:
                load_product(k, False)
            sp.wait_ge(out_ready, 1)
            sp.dma_start(out[0:(CH - 1) * P, :].rearrange("(c p) f -> p c f", p=P), result[:, 0:CH - 1, :]).then_inc(out_stored, 16)
            sp.dma_start(out[(CH - 1) * P:N, :], result[0:LAST, CH - 1, :]).then_inc(out_stored, 16)
            sp.wait_ge(out_stored, 32)

        @block.gpsimd
        def _(pool):
            pool.memset(x0[:, CH - 1, :], 0.0).then_inc(x_tail_zero, 1)
            pool.memset(ident[:, :], 0.0).then_inc(consts_step, 1)
            pool.memset(ident2[:, :], 0.0).then_inc(consts_step, 1)
            pool.wait_ge(consts_step, 2)
            pool.affine_select(out=ident[:, :], in_=ident[:, :], compare_op=ALU.not_equal, fill=1.0, base=0,
                               pattern=[[-1, P]], channel_multiplier=1).then_inc(consts_made, 1)
            pool.affine_select(out=ident2[:, :], in_=ident2[:, :], compare_op=ALU.not_equal, fill=1.0, base=0,
                               pattern=[[-1, F]], channel_multiplier=1).then_inc(consts_step, 1)
            pool.wait_ge(consts_step, 3)
            pool.affine_select(out=ident2[:, :], in_=ident2[:, :], compare_op=ALU.not_equal, fill=1.0, base=-F,
                               pattern=[[-1, F]], channel_multiplier=1).then_inc(consts_made, 1)
            ok = dict(allow_small_or_imprecise_dtypes=True)
            for out_, pattern, base, mul in (
                    (iota_b[:, :], [[1, 256]], 0, 0), (iota_f[:, :], [[1, P]], 0, 0), (win_base[:, :], [[WC, WINS]], 0, 0),
                    (first_dst[:, 0:WINS], [[WIN, WINS]], 0, 0), (last_dst[:, 0:WINS], [[WIN, WINS]], WIN - 1, 0),
                    (first_dst[:, WINS:RC], [[P, RC - WINS]], 0, 0), (last_dst[:, WINS:RC], [[P, RC - WINS]], P - 1, 0),
                    (chunk_base[:, :], [[P, STEPS]], 0, 0), (tile_no[:, :], [[P, TG]], 1, 1), (tile_left[:, :], [[-P, TG]], TP, -1)):
                pool.iota(out_, pattern, base=base, channel_multiplier=mul, **ok).then_inc(consts_made, 1)
            pool.memset(x_gathered[:, :, :], 1.0).then_inc(consts_step, 1)
            pool.memset(gathered[:, :, :], 1.0).then_inc(consts_step, 1)
            pool.memset(acc2[:, 0, :], 0.0).then_inc(consts_step, 1)
            pool.memset(acc2[:, 1:1 + CH, F:F + 1], 0.0).then_inc(consts_step, 1)
            pool.wait_ge(x_loaded, 32)
            pool.tensor_copy(acc2[:, 1:1 + CH, 0:F], x0[:, :, :]).then_inc(consts_step, 1)
            pool.memset(ones_row[:, :], 1.0).then_inc(consts_made, 1)
            pool.wait_ge(consts_step, 8)
            pool.wait_ge(tables_ready, 1)
            for b in range(YB):
                pool.wait_ge(y_stored[b], 16 * ((CH + YB - 1 - b) // YB))
            with pool.Fori(0, STEPS) as i:
                lo = range_of(pool, tab_lo, WINS + i, TP - TPC)
                for g in range(TPC // GG):
                    pool.wait_ge(rel_done, TPC * i + GG * g + GG)
                    pool.tensor_copy(gid_stage[:, GG * g:GG * g + GG], e_gid[:, bass.ds(lo + GG * g, GG)]).then_inc(ids_staged, 1)
                    pool.wait_ge(ids_staged, TPC // GG * i + g + 1)
                    pool.sem_inc(pool_passed, 1)
                    for s in range(GG * g, GG * g + GG):
                        pool.indirect_dma_start(
                            out=gathered[:, s, 0:F], out_offset=None, in_=y_dram[:, :],
                            in_offset=bass.IndirectOffsetOnAxis(ap=gid_stage[:, s:s + 1], axis=0)).then_inc(row_landed[s], 16)
                ex = range_of(pool, tab_ex, WINS + i, TP // XC)
                with pool.If(ex > 0):
                    cum = range_of(pool, tab_cum, WINS + i, STEPS * TP // XC)
                    with pool.Fori(0, ex) as trip:
                        pool.wait_ge(xd_done, cum + trip + 1)
                        pool.tensor_copy(x_gid_stage[:, :], e_gid[:, bass.ds(general_tile(pool, lo, TPC, trip, XC, XC), XC)]).then_inc(x_ids_staged, 1)
                        pool.wait_ge(x_ids_staged, cum + trip + 1)
                        pool.sem_inc(pool_passed, 1)
                        for q in range(XC):
                            pool.indirect_dma_start(
                                out=x_gathered[:, q, 0:F], out_offset=None, in_=y_dram[:, :],
                                in_offset=bass.IndirectOffsetOnAxis(ap=x_gid_stage[:, q:q + 1], axis=0)).then_inc(x_row_landed[q], 16)
                pool.sem_inc(pool_passed, 1)
            pool.sem_inc(pool_through, 1)

        @block.scalar
        def _(act):
            for q in range(-(-CH // 4)):
                n = min(4, CH - 4 * q) * P
                act.wait_ge(xt_put, q + 1)
                act.copy(xt[:, 512 * q:512 * q + n], ps[0:F, 4 + q % 2, 0:n]).then_inc(xt_copied, 1)
            u = 0
            for _, e_arr in EDGE_ARRAYS:
                for h in range(0, TG, 4):
                    n = min(4, TG - h) * P
                    act.wait_ge(edges_put, u + 1)
                    act.copy(e_arr[:, P * h:P * h + n], ps[:, 4 + u % 2, 0:n]).then_inc(edges_copied, 1)
                    u += 1
            for c in range(CH):
                act.wait_ge(y_put, c + 1)
                if c >= YB:
                    act.wait_ge(y_stored[c % YB], 16 * (c // YB))
                act.copy(y_rows[:, c % YB, :].rearrange("p (b n) -> p b n", b=2), ps[:, 2 * (c % 2):2 * (c % 2) + 2, :]).then_inc(y_copied, 1)
                act.wait_ge(y_copied, c + 1)
                act.dma_start(y_dram.rearrange("(c p r) f -> c p (r f)", p=P, r=RELS)[c], y_rows[:, c % YB, :]).then_inc(y_stored[c % YB], 16)
            act.wait_ge(tables_ready, 1)
            act.sem_inc(win_out, 3)
            act.sem_inc(keyw_ready, 1)

            def stage_window(n, slot):
                lo = range_of(act, tab_lo, n, TP - TPC)
                act.copy(e_stage[:, slot, :].rearrange("p (t k) -> p t k", k=3), e_all[:, bass.ds(lo, TPW), :]).then_inc(staged, 1)

            def put_out(n, j, turn):
                act.wait_ge(win_done, n + 4)
                act.copy(stage[:, bass.ds(turn, 1), :, :, j * WIN:(j + 1) * WIN].rearrange("p o m c d -> p (o m c) d"),
                         ps[:, SLOT[j], 0:2 * WC].rearrange("p (m d c) -> p m c d", m=2, c=CH)).then_inc(win_out, 1)

            for n in range(WPS - 1):
                stage_window(n, n)
            with act.Fori(0, STEPS) as i:
                turn = act.snap(i % 2)
                for j in range(WPS):
                    n = WPS * i + j
                    act.wait_ge(sel_ready, n + 1)
                    for s in range(TPW):
                        last = act.activation(key_w[:, SLOT[j], s, :], key_b[:, SLOT[j], s, 0:WC], ACT.Copy, scale=e_stage[:, j, 3 * s + 2:3 * s + 3])
                    last.then_inc(keyw_ready, 1)
                    act.wait_ge(keyw_ready, n + 1)
                    stage_window(n + WPS - 1, j - 1 if j else WPS - 1)
                    if j == 1:
                        act.wait_ge(blk_free, i + 1)
                    if j:
                        put_out(n - 1, j - 1, turn)
                put_out(WPS * i + WPS - 1, WPS - 1, turn)

            def sums(gg, p, g, width=GN):
                act.wait_ge(slice_used, CG * (gg + 1) + CG)
                act.copy(y_t[:, bass.ds(g * GN, width)], ps[:, BANK[p], 0:width]).then_inc(sum_copied, 1)

            def product(k):
                act.wait_ge(node_put, k)
                for p, g in enumerate(ORDER):
                    sums(GROUPS * k + p, p, g, LASTB * BLK if g == GROUPS - 1 else GN)

            def norm(n, squares):
                act.wait_ge(sq_in, n + 1)
                act.activation(squares[:, :, :], ln_c[:, :, :], ACT.Square).then_inc(sq_out, 1)
                act.wait_ge(var_in, n + 1)
                act.activation(ln_d[:, n, :], ln_v[:, n, :], ACT.Sqrt).then_inc(sd_out, 1)

            norm(0, x1)
            act.wait_ge(x_ready, 1)
            act.sem_inc(sum_copied, 2)
            for q in range(-(-CH // 4)):
                n = min(4, CH - 4 * q) * P
                act.wait_ge(x1t_put, q + 1)
                act.copy(x1t[:, 512 * q:512 * q + n], ps[0:F, 4 + q % 2, 0:n]).then_inc(x1t_copied, 1)
            with act.Fori(0, (GROUPS - 1) // 2) as it:
                for p in range(2):
                    sums(2 * it + p, p, 2 * it + p)
            sums(GROUPS - 1, GROUPS - 1, GROUPS - 1, LASTB * BLK)
            norm(1, cur)
            product(1)
            norm(2, cur)
            with act.Fori(2, KP) as k:
                act.wait_ge(x_ready, k + 1)
                act.copy(kept[:, bass.ds(k - 2, 1), :, :].rearrange("p o c f -> p (o c f)"), cur[:, :, :].rearrange(FLAT)).then_inc(cur_kept, 1)
                product(k)
            for u in range(14):
                n = min(4, CH - 4 * (u % 7)) * P
                act.wait_ge(ft_put, u + 1)
                if u >= 2:
                    act.wait_ge(fc_put, u - 1)
                act.copy(feats_t[:, u % 2, 0:n], ps[:, 2 + u % 2, 0:n]).then_inc(ft_copied, 1)
            norm(3, fc_sum)

        @block.vector
        def _(v):
            steps = [0]

            def link(ins):
                steps[0] += 1
                ins.then_inc(dve_step, 1)
                v.wait_ge(dve_step, steps[0])

            v.memset(dst_i[:, FULL_G, :], -1).then_inc(pads_set, 1)
            v.memset(src_i[:, FULL_G, :], 0).then_inc(pads_set, 1)
            v.memset(typ_i[:, FULL_G, :], 0).then_inc(pads_set, 1)
            v.memset(w_f[:, FULL_G, :], 0.0).then_inc(pads_set, 1)
            v.wait_ge(consts_made, 13)
            for n in range(4):
                v.wait_ge(main_loaded[n], 48)
            v.tensor_copy(scr_f[:, :, :], src_i[:, :, :])
            v.tensor_copy(scr2_f[:, :, :], typ_i[:, :, :])
            link(v.tensor_copy(dst_f[:, :, :], dst_i[:, :, :]))
            v.scalar_tensor_tensor(out=gid_f[:, :, :], in0=scr_f[:, :, :], scalar=float(RELS), in1=scr2_f[:, :, :], op0=ALU.mult, op1=ALU.add)
            v.tensor_scalar(tmp_i[:, :, :], src_i[:, :, :], P - 1, None, ALU.bitwise_and)
            link(v.tensor_scalar(hi_i[:, :, :], src_i[:, :, :], 7, None, ALU.arith_shift_right))
            v.tensor_copy(lo_f[:, :, :], tmp_i[:, :, :])
            link(v.tensor_copy(scr_f[:, :, :], hi_i[:, :, :]))
            v.scalar_tensor_tensor(out=key_f[:, :, :], in0=dst_f[:, :, :], scalar=float(CH), in1=scr_f[:, :, :], op0=ALU.mult, op1=ALU.add).then_inc(edges_ready, 1)
            v.tensor_reduce(t_max[:, :], dst_f[:, :, :], axis=AX.X, op=ALU.max)
            link(v.tensor_scalar(scr2_f[:, :, :], dst_f[:, :, :], 0.0, 5000.0, ALU.is_lt, ALU.mult))
            link(v.tensor_tensor(scr_f[:, :, :], scr2_f[:, :, :], dst_f[:, :, :], ALU.add))
            v.tensor_reduce(t_min[:, :], scr_f[:, :, :], axis=AX.X, op=ALU.min)
            v.memset(r_zero[:, :], 0.0)
            link(v.memset(best[:, :, 0, :], 0.0))
            for h in range(TG):
                last = v.tensor_scalar(has_a[:, h, :], last_dst[:, :], t_min[:, h:h + 1], None, ALU.is_ge)
            link(last)
            for h in range(TG):
                last = v.scalar_tensor_tensor(out=has[:, h, :], in0=first_dst[:, :], scalar=t_max[:, h:h + 1], in1=has_a[:, h, :], op0=ALU.is_le, op1=ALU.mult)
            link(last)
            for h in range(TG):
                a, b = h % 2, (h + 1) % 2
                v.scalar_tensor_tensor(out=best[:, 0, b, :], in0=has[:, h, :], scalar=tile_left[:, h:h + 1], in1=best[:, 0, a, :], op0=ALU.mult, op1=ALU.max)
                link(v.scalar_tensor_tensor(out=best[:, 1, b, :], in0=has[:, h, :], scalar=tile_no[:, h:h + 1], in1=best[:, 1, a, :], op0=ALU.mult, op1=ALU.max))
            v.sem_inc(best_ready, 1)
            v.wait_ge(small_put, 1)
            v.tensor_copy(wa2_t[:, :], ps[:, 6, 0:F])
            v.tensor_copy(wb_t[:, :], ps[0:F, 6, F:2 * F])
            v.tensor_copy(fc_t[:, :, :], ps[:, 6, 128:128 + 3 * F].rearrange("p (j f) -> p j f", f=F)).then_inc(fc_step, 1)
            v.wait_ge(fc_step, 1)
            v.tensor_tensor(fc_t[0:F, 1, :], fc_t[0:F, 1, :], ps[0:F, 6, 128 + 3 * F:128 + 4 * F], ALU.add).then_inc(fc_step, 1)
            v.tensor_copy(small[:, :], ps[:, 7, 0:2 * F + 1]).then_inc(small_copied, 1)
            v.wait_ge(best_put, 1)
            v.tensor_reduce(range_red[:, :, :], ps[:, 6:8, 0:RC].rearrange("p m (b t) -> p m b t", t=P), axis=AX.X, op=ALU.max).then_inc(range_ready, 1)
            v.wait_ge(range_put, 1)
            v.tensor_copy(range_t[:, :], ps[0:6, 6, 0:P]).then_inc(range_turned, 1)
            v.wait_ge(range_back, 16)
            link(v.tensor_scalar(r_a[:, :], r_red[:, 0, :], -1.0, float(TP), ALU.mult, ALU.add))
            link(v.tensor_scalar(r_lo[:, :], r_a[:, :], float(TP - TPC), None, ALU.min))
            v.tensor_copy(tab_lo[:, :], r_lo[:, :])
            link(v.tensor_tensor(r_k[:, :], r_red[:, 1, :], r_lo[:, :], ALU.subtract))
            for a, b, done, trip in ((0, WINS, TPW, XT), (WINS, RC, TPC, XC)):
                link(v.tensor_scalar(r_a[:, a:b], r_k[:, a:b], -float(done), 0.0, ALU.add, ALU.max))
                link(v.tensor_scalar(r_k[:, a:b], r_a[:, a:b], float(trip - 1), None, ALU.add))
                link(v.tensor_copy(r_ki[:, a:b], r_k[:, a:b]))
                link(v.tensor_scalar(tab_ex[:, a:b], r_ki[:, a:b], trip.bit_length() - 1, None, ALU.arith_shift_right))
                link(v.tensor_copy(r_ex[:, a:b], tab_ex[:, a:b]))
                link(v.tensor_tensor_scan(r_cum[:, a:b], r_ex[:, a:b], r_zero[:, a:b], 0.0, ALU.add, ALU.add))
                link(v.tensor_tensor(r_a[:, a:b], r_cum[:, a:b], r_ex[:, a:b], ALU.subtract))
            v.tensor_copy(tab_cum[:, :], r_a[:, :])
            v.tensor_reduce(tab_any[:, :], r_ex[:, 0:WINS].rearrange("o (i j) -> o i j", j=WPS), axis=AX.X, op=ALU.max).then_inc(tables_ready, 1)
            v.wait_ge(tables_ready, 1)

            v.sem_inc(dsel_ready, DB)
            for b in range(YB):
                v.wait_ge(y_stored[b], 16 * ((CH + YB - 1 - b) // YB))

            def window_slow(i, j, turn):
                n = v.snap(WPS * i + j)
                ex = range_of(v, tab_ex, n, TP // XT)
                with v.If(ex > 0):
                    cum = range_of(v, tab_cum, n, WINS * TP // XT)
                    lo = range_of(v, tab_lo, n, TP - TPC)
                    with v.Fori(0, ex) as trip:
                        t = general_tile(v, lo, TPW, trip, XT, XT)
                        for q in range(XT):
                            v.tensor_scalar(x_key_b[:, q, :], iota_b[:, 0:WS], win_base[:, bass.ds(n, 1)], e_all[:, bass.ds(t + q, 1), 1], ALU.add, ALU.is_equal)
                            v.tensor_scalar(x_sel_b[:, q, :], iota_b[:, 0:P], e_all[:, bass.ds(t + q, 1), 0], None, ALU.is_equal)
                            last = v.tensor_scalar(x_sel_f[:, q, :], iota_f[:, :], e_all[:, bass.ds(t + q, 1), 0], None, ALU.is_equal)
                        last.then_inc(xb_ready, 1)
                        v.wait_ge(xb_ready, cum + trip + 1)
                        for q in range(XT):
                            last = v.tensor_scalar(x_key_w[:, q, :], x_key_b[:, q, :], e_all[:, bass.ds(t + q, 1), 2], None, ALU.mult)
                        last.then_inc(xs_ready, 1)
                        v.wait_ge(x_done, cum + trip + 1)
                        for m in range(2):
                            a = stage[:, bass.ds(turn, 1), m, :, bass.ds(WIN * j, WIN)].rearrange("p o c d -> p (o c) d")
                            last = v.tensor_tensor(a, a, ps[:, 7, WS * m:WS * m + WC].rearrange("p (d c) -> p c d", c=CH), ALU.add)
                        last.then_inc(x_added, 1)
                        v.wait_ge(x_added, cum + trip + 1)
                        v.sem_inc(dve_passed, 1)
                v.sem_inc(dve_passed, 1)

            with v.Fori(0, STEPS) as i:
                lo = range_of(v, tab_lo, WINS + i, TP - TPC)
                v.wait_ge(dsel_ready, DB * i + DB)
                v.tensor_scalar(dst_stage[:, :], e_dst[:, bass.ds(lo, TPC)], chunk_base[:, bass.ds(i, 1)], None, ALU.subtract).then_inc(dst_staged, 1)
                for j in range(WPS):
                    n = WPS * i + j
                    base = win_base[:, bass.ds(n, 1)]
                    v.wait_ge(staged, n + 1)
                    v.wait_ge(win_done, n + 1)
                    v.tensor_tensor(sel_f[:, SLOT[j], :, :], iota_f[:, :].unsqueeze(1).to_broadcast([P, TPW, P]),
                                    e_stage[:, j, 0:3 * TPW:3].unsqueeze(2).to_broadcast([P, TPW, P]), ALU.is_equal).then_inc(self_ready, 1)
                    for s in range(TPW):
                        last = v.tensor_scalar(key_b[:, SLOT[j], s, :], iota_b[:, 0:WS], base, e_stage[:, j, 3 * s + 1:3 * s + 2], ALU.add, ALU.is_equal)
                    last.then_inc(sel_ready, 1)
                    v.wait_ge(self_ready, n + 1)
                    v.tensor_copy(sel_b[:, SLOT[j], :, :], sel_f[:, SLOT[j], :, :]).then_inc(selb_ready, 1)
                    if j == 1:
                        v.wait_ge(rel_done, TPC * i + TPC)
                        v.tensor_tensor(acc[:, bass.ds(i, 1), :].rearrange(FLAT), ps[:, 6, 0:D1], acc2[:, bass.ds(i, 1), :].rearrange(FLAT), ALU.add).then_inc(rel_out, 1)
                        v.wait_ge(dst_staged, i + 1)
                    if AFTER[j]:
                        a, b = AFTER[j][0], AFTER[j][-1] + 1
                        v.wait_ge(rel_done, TPC * i + b)
                        v.tensor_tensor(dsel[:, a:b, :], iota_f[:, :].unsqueeze(1).to_broadcast([P, b - a, P]),
                                        dst_stage[:, a:b].unsqueeze(2).to_broadcast([P, b - a, P]), ALU.is_equal).then_inc(dsel_ready, 1)
                some = range_of(v, tab_any, i, TP // XT)
                with v.If(some > 0):
                    v.wait_ge(win_out, WPS * i + WPS + 3)
                    v.sem_inc(dve_passed, 1)
                    turn = v.snap(i % 2)
                    with v.Fori(0, WPS) as j:
                        window_slow(i, j, turn)
                v.sem_inc(step_done, 1)
                ex = range_of(v, tab_ex, WINS + i, TP // XC)
                with v.If(ex > 0):
                    cum = range_of(v, tab_cum, WINS + i, STEPS * TP // XC)
                    with v.Fori(0, ex) as trip:
                        t = general_tile(v, lo, TPC, trip, XC, XC)
                        for q in range(XC):
                            last = v.tensor_scalar(x_dsel[:, q, :], iota_f[:, :], chunk_base[:, bass.ds(i, 1)], e_dst[:, bass.ds(t + q, 1)], ALU.add, ALU.is_equal)
                        last.then_inc(xd_ready, 1)
                        v.wait_ge(xd_done, cum + trip + 2)
                        a = acc2[:, bass.ds(i + 1, 1), :].rearrange(FLAT)
                        v.tensor_tensor(a, a, ps[:, 7, 0:D1], ALU.add).then_inc(xd_added, 1)
                        v.wait_ge(xd_added, cum + trip + 1)
                        v.sem_inc(dve_passed, 1)
                v.sem_inc(dve_passed, 1)
            v.wait_ge(rel_done, TPC * STEPS + TPC)
            link(v.tensor_tensor(acc[:, STEPS, :], ps[:, 6, 0:D1], acc2[:, STEPS, :], ALU.add))
            v.wait_ge(win_out, WINS + 3)
            v.wait_ge(win_done, WINS + 3)
            v.wait_ge(pe_through, 1)
            v.wait_ge(pool_through, 1)

            def bcast(m):
                return m.unsqueeze(2).to_broadcast([P, CH, F])

            def norm(n, h, squares, x_out):
                link(v.tensor_reduce(ln_s[:, n, :], h, axis=AX.X, op=ALU.add))
                link(v.tensor_scalar(ln_m[:, n, :], ln_s[:, n, :], 1.0 / F, None, ALU.mult))
                v.tensor_tensor(ln_c[:, :, :], h, bcast(ln_m[:, n, :]), ALU.subtract).then_inc(sq_in, 1)
                v.wait_ge(sq_out, n + 1)
                link(v.tensor_reduce(ln_s[:, n, :], squares[:, :, :], axis=AX.X, op=ALU.add))
                v.tensor_scalar(ln_v[:, n, :], ln_s[:, n, :], 1.0 / F, EPS, ALU.mult, ALU.add).then_inc(var_in, 1)
                v.wait_ge(sd_out, n + 1)
                link(v.reciprocal(ln_r[:, n, :], ln_d[:, n, :]))
                return v.tensor_tensor(x_out[:, :, :], ln_c[:, :, :], bcast(ln_r[:, n, :]), ALU.mult)

            node_sums = ps[:, 2:6, :].rearrange("p b n -> p (b n)")[:, 0:CH * F].rearrange("p (c f) -> p c f", f=F)
            v.tensor_scalar(deg[:, :], acc[:, 1:1 + CH, F], 1.0, None, ALU.max).then_inc(deg_ready, 1)
            v.wait_ge(deg_ready, 1)
            v.reciprocal(rdeg[:, :], deg[:, :])
            norm(0, acc[:, 1:1 + CH, 0:F], x1, x1).then_inc(x_ready, 1)
            v.wait_ge(node_put, 1)
            v.wait_ge(x_ready, 1)
            link(v.tensor_tensor(ln_h[:, :, :], node_sums, bcast(rdeg[:, :]), ALU.mult))
            own = [ps[:, b, :].rearrange("p (c f) -> p c f", f=F) for b in (6, 7, 0, 1)]
            for i, b in enumerate(own):
                n = min(8, CH - 8 * i)
                last = v.tensor_tensor(ln_c[:, 8 * i:8 * i + n, :], b[:, 0:n, :], x1[:, 8 * i:8 * i + n, :], ALU.add)
            link(last)
            v.tensor_tensor(cur[:, :, :], ln_c[:, :, :], small[:, 0:F].unsqueeze(1).to_broadcast([P, CH, F]), ALU.add).then_inc(node_free, 1)
            v.wait_ge(node_free, 1)
            link(v.tensor_tensor(ln_h[:, :, :], ln_h[:, :, :], cur[:, :, :], ALU.add))
            norm(1, ln_h[:, :, :], cur, cur).then_inc(x_ready, 1)
            v.wait_ge(node_put, 2)
            v.wait_ge(x_ready, 2)
            v.tensor_tensor(ln_h[:, :, :], node_sums, cur[:, :, :], ALU.add).then_inc(node_free, 1)
            v.wait_ge(node_free, 2)
            norm(2, ln_h[:, :, :], cur, cur).then_inc(x_ready, 1)
            def pair(j, parts):
                for i, (a, b) in enumerate(parts):
                    v.tensor_tensor(diffs[:, i, :, :], a[:, :, :], b[:, :, :], ALU.subtract).then_inc(diff_ready, 1)
                for i in range(2):
                    v.wait_ge(diff_ready, 2 * j + i + 1)
                    v.scalar_tensor_tensor(out=feats[:, j, :, i, :], in0=diffs[:, i, :, :], scalar=-1.0, in1=diffs[:, i, :, :], op0=ALU.mult, op1=ALU.max).then_inc(feats_ready, 1)

            for k in range(2, KP):
                v.wait_ge(node_put, k + 1)
                v.wait_ge(cur_kept, k - 1)
                if k == 2:
                    v.wait_ge(x_ready, 3)
                v.tensor_copy(cur[:, :, :], node_sums).then_inc(x_ready, 1)
            v.wait_ge(x_ready, 7)
            u4 = cur
            pair(0, ((u1, u2), (u3, u2)))
            v.wait_ge(feats_ready, 2)
            pair(1, ((u2, u4), (u4, u3)))
            v.wait_ge(fc_put, 14)
            v.wait_ge(feats_ready, 4)
            fc_sums = [ps[:, b, :].rearrange("p (c f) -> p c f", f=F) for b in (0, 1, 6, 7)]
            for i, b in enumerate(fc_sums):
                n = min(8, CH - 8 * i)
                last = v.tensor_tensor(fc_out[:, 8 * i:8 * i + n, :], b[:, 0:n, :], small[:, F:2 * F].unsqueeze(1).to_broadcast([P, n, F]), ALU.add)
            link(last)
            v.tensor_scalar(fc_neg[:, :, :], fc_out[:, :, :], 0.0, small[:, 2 * F:2 * F + 1], ALU.min, ALU.mult)
            link(v.scalar_tensor_tensor(out=fc_sum[:, :, :], in0=fc_out[:, :, :], scalar=0.0, in1=x3[:, :, :], op0=ALU.max, op1=ALU.add))
            link(v.tensor_tensor(ln_h[:, :, :], fc_sum[:, :, :], fc_neg[:, :, :], ALU.add))
            norm(3, ln_h[:, :, :], fc_sum, result).then_inc(out_ready, 1)

        @block.tensor
        def _(pe):
            def transposed(x, put, copied, wait_first):
                for q in range(-(-CH // 4)):
                    if q >= 2:
                        pe.wait_ge(copied, q - 1)
                    for c in range(4 * q, min(4 * q + 4, CH)):
                        last = pe.transpose(ps[0:F, 4 + q % 2, P * (c % 4):P * (c % 4) + P], x[:, c, :], ident[:, :])
                    last.then_inc(put, 1)

            pe.wait_ge(consts_made, 13)
            pe.wait_ge(x_loaded, 32)
            transposed(x0, xt_put, xt_copied, None)
            pe.wait_ge(edges_ready, 1)
            u = 0
            for f_arr, _ in EDGE_ARRAYS:
                for h in range(0, TG, 4):
                    if u >= 2:
                        pe.wait_ge(edges_copied, u - 1)
                    elif u == 0:
                        pe.wait_ge(xt_copied, -(-CH // 4))
                    for g in range(h, min(h + 4, TG)):
                        last = pe.transpose(ps[:, 4 + u % 2, P * (g - h):P * (g - h) + P], f_arr[:, g, :], ident[:, :])
                    last.then_inc(edges_put, 1)
                    u += 1
            pe.wait_ge(w_loaded, 16 * 12)
            pe.transpose(ps[:, 6, 0:F], l1_rows[:, 0:2, :].rearrange(FLAT), ident[0:F, 0:F])
            pe.transpose(ps[0:F, 6, F:2 * F], l1_rows[:, 2, :], ident[0:F, 0:F])
            for j in range(3):
                pe.transpose(ps[:, 6, 128 + F * j:128 + F * j + F], fc_rows[:, P * j:P * j + P], ident[0:F, 0:F])
            pe.transpose(ps[0:F, 6, 128 + 3 * F:128 + 4 * F], fc_rows[:, 6 * F:7 * F], ident[0:F, 0:F])
            pe.matmul(ps[:, 7, 0:2 * F + 1], ones_row[:, :], small_row[:, :], start=True, stop=True).then_inc(small_put, 1)
            def ranges():
                pe.wait_ge(best_ready, 1)
                pe.wait_ge(small_copied, 1)
                for m in range(2):
                    for b in range(3):
                        last = pe.transpose(ps[:, 6 + m, P * b:P * b + P], best[:, m, TG % 2, P * b:P * b + P], ident[:, :])
                last.then_inc(best_put, 1)
                pe.wait_ge(range_ready, 1)
                pe.transpose(ps[0:6, 6, 0:P], range_red[:, :, :].rearrange(FLAT), ident[:, :]).then_inc(range_put, 1)

            pe.wait_ge(rel_loaded, 16)
            for c in range(CH):
                if c == 8:
                    ranges()
                pe.wait_ge(xt_copied, c // 4 + 1)
                if c >= 2:
                    pe.wait_ge(y_copied, c - 1)
                for i in range(2):
                    last = pe.matmul(ps[:, 2 * (c % 2) + i, :], xt[:, c * P:c * P + P], rel_sb[:, 8 * i:8 * i + 8, :].rearrange("i r o -> i (r o)"), start=True, stop=True)
                last.then_inc(y_put, 1)
            pe.wait_ge(tables_ready, 1)
            pe.sem_inc(win_done, 3)
            pe.sem_inc(rel_done, TPC)
            pe.sem_inc(xd_done, 1)
            with pe.Fori(0, STEPS) as i:
                for j in range(WPS):
                    n = WPS * i + j
                    pe.wait_ge(selb_ready, n + 1)
                    pe.wait_ge(keyw_ready, n + 2)
                    pe.wait_ge(win_out, n + 1)
                    for s in range(TPW):
                        pe.matmul(ps[:, SLOT[j], 0:WC], sel_f[:, SLOT[j], s, :], key_w[:, SLOT[j], s, :], start=(s == 0), stop=(s == TPW - 1))
                    for s in range(TPW):
                        last = pe.matmul(ps[:, SLOT[j], WC:2 * WC], sel_b[:, SLOT[j], s, :], key_b[:, SLOT[j], s, 0:WC], start=(s == 0), stop=(s == TPW - 1))
                    last.then_inc(win_done, 1)
                    if AFTER[j]:
                        pe.wait_ge(dsel_ready, DB * i + DB + j - 1)
                    for s in AFTER[j]:
                        pe.wait_ge(row_landed[s], 16 * i + 16)
                        if s == 0:
                            pe.wait_ge(rel_out, i + 1)
                        pe.matmul(ps[:, 6, 0:D1], dsel[:, s, :], gathered[:, s, :], start=(s == 0), stop=(s == TPC - 1)).then_inc(rel_done, 1)
                some = range_of(pe, tab_any, i, TP // XT)
                with pe.If(some > 0):
                    with pe.Fori(0, WPS) as j:
                        n = pe.snap(WPS * i + j)
                        ex = range_of(pe, tab_ex, n, TP // XT)
                        with pe.If(ex > 0):
                            cum = range_of(pe, tab_cum, n, WINS * TP // XT)
                            with pe.Fori(0, ex) as trip:
                                pe.wait_ge(xs_ready, cum + trip + 1)
                                for q in range(XT):
                                    pe.matmul(ps[:, 7, 0:WC], x_sel_f[:, q, :], x_key_w[:, q, 0:WC], start=(q == 0), stop=(q == XT - 1))
                                for q in range(XT):
                                    last = pe.matmul(ps[:, 7, WS:WS + WC], x_sel_b[:, q, :], x_key_b[:, q, 0:WC], start=(q == 0), stop=(q == XT - 1))
                                last.then_inc(x_done, 1)
                        pe.sem_inc(pe_passed, 1)
                ex = range_of(pe, tab_ex, WINS + i, TP // XC)
                with pe.If(ex > 0):
                    cum = range_of(pe, tab_cum, WINS + i, STEPS * TP // XC)
                    with pe.Fori(0, ex) as trip:
                        pe.wait_ge(xd_ready, cum + trip + 1)
                        for q in range(XC):
                            pe.wait_ge(x_row_landed[q], (cum + trip) * 16 + 16)
                            last = pe.matmul(ps[:, 7, 0:D1], x_dsel[:, q, :], x_gathered[:, q, :], start=(q == 0), stop=(q == XC - 1))
                        last.then_inc(xd_done, 1)
                pe.sem_inc(pe_passed, 1)
            pe.sem_inc(pe_through, 1)

            pe.wait_ge(x_ready, 1)
            transposed(x1, x1t_put, x1t_copied, None)
            pe.sem_inc(slice_used, CG)

            def column_group(gg, p, x, slices, blocks, landed_by):
                pe.wait_ge(sum_copied, gg + 1)
                for cg in range(CG):
                    landed_by(cg)
                    m = slices[:, cg, :].rearrange("p (b c d) -> p b c d", b=GB, d=BLK)
                    for ci in range(CI):
                        c = cg * CI + ci
                        o = ps[F * (c % 2):F * (c % 2) + F, BANK[p], 0:blocks * BLK].rearrange("p (b d) -> p b d", d=BLK)
                        last = pe.matmul(o, x[:, c, :], m[:, 0:blocks, ci, :], start=(c < 2), stop=(c >= CH - 2))
                    last.then_inc(slice_used, 1)

            def streamed(use):
                return lambda cg: pe.wait_ge(landed[cg], 16 * use + 16)

            def by_nodes(k, rhs):
                pe.wait_ge(sum_copied, GROUPS * (k + 1) + 2)
                for c in range(CH):
                    last = pe.matmul(ps[:, 2 + c // 8, F * (c % 8):F * (c % 8) + F], y_t[:, c * P:c * P + P], rhs, start=True, stop=True)
                return last

            with pe.Fori(0, (GROUPS - 1) // 2) as it:
                for p in range(2):
                    column_group(2 * it + p, p, x1, ring, GB, streamed(2 * it + p))
            column_group(GROUPS - 1, GROUPS - 1, x1, ring, LASTB, streamed(GROUPS - 1))
            by_nodes(0, wa2_t[:, :])
            pe.wait_ge(x1t_copied, -(-CH // 4))
            for c in range(CH):
                b = (6, 7, 0, 1)[c // 8]
                last = pe.matmul(ps[:, b, F * (c % 8):F * (c % 8) + F], x1t[:, c * P:c * P + P], wb_t[:, :], start=True, stop=True)
            last.then_inc(node_put, 1)
            with pe.Fori(1, KP) as k:
                pe.wait_ge(x_ready, k + 1)
                for p, g in enumerate(ORDER):
                    gg = GROUPS * k + p
                    if p in STREAMED:
                        column_group(gg, p, cur, ring, LASTB if g == GROUPS - 1 else GB, streamed(GROUPS + len(STREAMED) * (k - 1) + STREAMED.index(p)))
                    else:
                        column_group(gg, p, cur, resident[:, CG * g:CG * g + CG, :], GB,
                                     lambda cg: pe.wait_ge(resident_landed[g], 16 * CG) if cg == 0 else None)
                by_nodes(k, ident2[:, :]).then_inc(node_put, 1)
            def fc_place(c):
                return ps[:, (0, 1, 6, 7)[c // 8], F * (c % 8):F * (c % 8) + F]

            pe.wait_ge(sum_copied, GROUPS * KP + 2)
            for c in range(CH):
                pe.matmul(fc_place(c), y_t[:, c * P:c * P + P], fc_t[:, 0, :], start=(c % 8 == 0), stop=False, skip_group_check=True)

            def chunks(u):
                return range(4 * (u % 7), min(4 * (u % 7) + 4, CH))

            pe.wait_ge(x_ready, KP + 1)
            for u in range(15):
                if u < 14:
                    if u % 7 == 0:
                        pe.wait_ge(feats_ready, 2 * (u // 7) + 2)
                    if u >= 2:
                        pe.wait_ge(ft_copied, u - 1)
                    for c in chunks(u):
                        last = pe.transpose(ps[:, 2 + u % 2, P * (c % 4):P * (c % 4) + P], feats[:, u // 7, c, :, :].rearrange(FLAT), ident[:, :])
                    last.then_inc(ft_put, 1)
                if u:
                    w = u - 1
                    pe.wait_ge(ft_copied, w + 1)
                    for c in chunks(w):
                        last = pe.matmul(fc_place(c), feats_t[:, w % 2, P * (c % 4):P * (c % 4) + P], fc_t[:, 1 + w // 7, :],
                                         start=False, stop=(w >= 7), skip_group_check=True)
                    last.then_inc(fc_put, 1)


_INS = [("x", "x"), ("src", "src"), ("dst", "dst"), ("edge_type_16", "type"), ("edge_weight", "weight"),
        ("L0_gnn_weight", "rel_w"), ("L1_gnn_W", "l1_w"), ("L1_gnn_b", "l1_b"), ("L3_gnn_fc_w", "fc_w"),
        ("L3_gnn_bias", "fc_b"), ("L3_gnn_prelu_a", "prelu_a")]


def kernel(**inputs):
    import numpy as np
    import concourse.bacc as bacc
    from concourse import mybir as _mybir
    from concourse.bass_utils import run_bass_kernel_spmd as run

    nc = bacc.Bacc("TRN2", target_bir_lowering=False, num_devices=1)
    arrays, args = {}, []
    for name, short in _INS:
        a = np.ascontiguousarray(inputs[name])
        if a.ndim == 0:
            a = a.reshape(1)
        arrays[short] = a
        args.append(nc.dram_tensor(short, a.shape, _mybir.dt.from_np(a.dtype), kind="ExternalInput").ap())
    out = nc.dram_tensor("out", (N, F), F32, kind="ExternalOutput").ap()
    build(nc, *args, out)
    r = run(nc, [arrays], core_ids=[0])
    return r.results[0]["out"]
```

```python
import concourse.bass as bass
import concourse.mybir as mybir
from contextlib import ExitStack

F32 = mybir.dt.float32
BF16 = mybir.dt.bfloat16
I32 = mybir.dt.int32
ALU = mybir.AluOpType
ACT = mybir.ActivationFunctionType
AX = mybir.AxisListType

P = 128
N = 3125
E = 103125
F = 64
RELS = 16
EPS = 1e-5

CH = -(-N // P)
PC = N // CH
DIV_MUL, DIV_SHIFT = 4195, 19
assert CH * PC == N and N * DIV_MUL < 1 << 24 and all(n * DIV_MUL >> DIV_SHIFT == n // PC for n in range(N))
TILES = -(-E // P)
TG = -(-TILES // P)
TP = TG * P
FULL_G = E // (P * P)
REST_T = (E - FULL_G * P * P) // P
REST_E = E - (FULL_G * P + REST_T) * P

WIN = 10
WC = WIN * CH
WS = WC + 2
TPW = 4
STEPS = CH
WPS = -(-PC // WIN)
NARROW = WPS * WIN - PC
START = [WIN * j - min(j, NARROW) for j in range(WPS + 1)]
WINS = STEPS * WPS
BLK = PC
TPC = 34
GG = 7
XT = 8
XC = 4
RC = 3 * P
SLOTS = 4
SLOT = [j % 3 for j in range(WPS - 1)] + [3]
LATE = 13
AFTER = [[] for _ in range(2)] + [list(range((TPC - LATE) * j // (WPS - 3), (TPC - LATE) * (j + 1) // (WPS - 3))) for j in range(WPS - 3)] + [list(range(TPC - LATE, TPC))]
DB = WPS - 2
assert WPS % 3 == 1 and WINS + STEPS <= RC and TILES + XC + TPC < TP

YB = 4
GB = 3
GROUPS = -(-STEPS // GB)
GN = GB * BLK
LASTB = STEPS - (GROUPS - 1) * GB
COLS = STEPS * BLK
CG = 5
CI = CH // CG
SL = CI * BLK
RES = 3
ORDER = [3, 0, 4, 1, 5, 2, 6, 7, 8]
BANK = [0, 1] * ((GROUPS - 1) // 2) + [6]
HALVES = [(0, CH // 2), (CH // 2, CH)]
FIRST = 16
STREAMED = [p for p, g in enumerate(ORDER) if g >= RES]
assert sorted(ORDER[:-2]) == list(range(GROUPS - 2)) and FIRST * PC + P - PC <= GB * BLK * (GROUPS - 2)
assert GROUPS % 2 == 1 and ORDER[-1] == GROUPS - 1
D1 = F + 1


def build(nc, x_in, src_in, dst_in, type_in, weight_in, rel_w, l1_w, l1_b, fc_w, fc_b, prelu_a, out):
    with ExitStack() as ctx:
        def sb(name, shape, dt=F32):
            return ctx.enter_context(nc.sbuf_tensor(name, shape, dt))

        def sem(name):
            return ctx.enter_context(nc.semaphore(name))

        class Part:

            def __init__(self, whole, start, end):
                self.tensor, self.start, self.at, self.size = whole.tensor, start, start, end

            def restart(self):
                self.at = self.start

            def take(self, shape, dt=F32):
                count = 1
                for n in shape[1:]:
                    count *= n
                words = -(-count * (2 if dt == BF16 else 4) // 4)
                a = self.tensor[0:shape[0], self.at // 4:self.at // 4 + words]
                self.at += 4 * words
                assert self.at <= self.size, (self.at, self.size)
                a = a if dt == F32 else a.bitcast(dt)
                if len(shape) == 3:
                    a = a.rearrange("p (a b) -> p a b", b=shape[2])
                if len(shape) == 4:
                    a = a.rearrange("p (a b c) -> p a b c", b=shape[2], c=shape[3])
                if len(shape) == 5:
                    a = a.rearrange("p (a b c d) -> p a b c d", b=shape[2], c=shape[3], d=shape[4])
                return a

        class Arena(Part):
            def __init__(self, name, size):
                self.start, self.at, self.size = 0, 0, size
                self.tensor = sb(name, [P, size // 4])

        slice_bytes, node_bytes = GB * SL * 4, CH * F * 4
        body = Arena("body", (1 + RES) * CG * slice_bytes + 5 * node_bytes)
        PREP = 75400
        prep, loop = Part(body, 0, PREP), Part(body, PREP, body.size)

        y_dram = nc.dram_tensor("rel_rows", (CH * P * RELS, F), F32, kind="Internal").ap()

        def matrix(name):
            return (nc.dram_tensor(name, (GROUPS - 1, CG, P, GB * SL), F32, kind="Internal").ap(),
                    nc.dram_tensor(name + "_last", (CG, P, LASTB * SL), F32, kind="Internal").ap())

        weights_t, counts_t = matrix("weights_t"), matrix("counts_t")
        range_dram = nc.dram_tensor("ranges", (6, P), F32, kind="Internal").ap()

        ident = sb("ident", [P, P])
        ident2 = sb("ident2", [P, F])
        wa2_t = sb("wa2_t", [P, F])
        wb_t = sb("wb_t", [F, F])
        fc_t = sb("fc_t", [P, 3, F])
        small = sb("small", [P, 2 * F + 1])
        src_i = prep.take([P, TG, P], I32)
        dst_i = prep.take([P, TG, P], I32)
        typ_i = prep.take([P, TG, P], I32)
        tmp_i = prep.take([P, TG, P], I32)
        tmp2_i = prep.take([P, TG, P], I32)
        src_f = prep.take([P, TG, P])
        hi_f = prep.take([P, TG, P])
        w_f = prep.take([P, TG, P])
        dst_f = prep.take([P, TG, P])
        lo_f = prep.take([P, TG, P])
        key_f = prep.take([P, TG, P])
        gid_f = prep.take([P, TG, P])
        scr_f = prep.take([P, TG, P])
        scr2_f = prep.take([P, TG, P])
        has_a = prep.tensor[:, 0:TG * RC].rearrange("p (a b) -> p a b", b=RC)
        assert RC <= 3 * P
        has_start = prep.at
        has = prep.take([P, TG, RC])
        best = prep.take([P, 2, 2, RC])
        tile_no = prep.take([P, TG])
        tile_left = prep.take([P, TG])
        t_min = prep.take([P, TG])
        t_max = prep.take([P, TG])
        first_dst = prep.take([P, RC])
        last_dst = prep.take([P, RC])
        range_red = prep.take([P, 2, 3])
        range_t = prep.take([6, P])
        e_all = loop.take([P, TP, 3])
        e_dst = loop.take([P, TP])
        e_gid = loop.take([P, TP], I32)
        r_zero = prep.take([1, RC])
        prep.at = has_start
        r_red = prep.take([1, 2, RC])
        r_a, r_lo, r_k, r_ex, r_cum = [prep.take([1, RC]) for _ in range(5)]
        r_ki = prep.take([1, RC], I32)
        sel_start = loop.at
        sel_f = loop.take([P, SLOTS, TPW, P])
        sel_b = loop.take([P, SLOTS, TPW, P], BF16)
        key_b = loop.take([P, SLOTS, TPW, WS], BF16)
        key_w_start = loop.at
        key_w = loop.take([P, SLOTS, TPW, WC])
        dst_stage = loop.take([P, TPC])
        dsel_start = loop.at
        dsel = loop.take([P, TPC, P])
        prep.restart()
        stage = prep.take([P, 2, 2, CH, BLK])
        x_sel_f = prep.take([P, XT, P])
        x_sel_b = prep.take([P, XT, P], BF16)
        x_key_b = prep.take([P, XT, WS], BF16)
        x_key_w = prep.take([P, XT, WS])
        x_dsel = prep.take([P, XC, P])
        gathered = loop.take([P, TPC, D1])
        x_gathered = loop.take([P, XC, D1])
        iota_b = loop.take([P, 256], BF16)
        iota_f = loop.take([P, P])
        win_base = loop.take([P, WINS])
        chunk_base = loop.take([P, STEPS])
        ones_row = loop.take([1, P])
        tab_lo = loop.take([1, RC], I32)
        tab_ex = loop.take([1, RC], I32)
        tab_cum = loop.take([1, RC], I32)
        tab_win = loop.take([1, STEPS], I32)
        tab_any = loop.take([1, STEPS], I32)
        e_stage = loop.take([P, WPS, TPW * 3])
        gid_stage = loop.take([P, TPC], I32)
        x_gid_stage = loop.take([P, XC], I32)
        acc_start = loop.at
        acc = loop.take([P, 1 + STEPS, D1])
        acc2 = loop.take([P, 1 + STEPS, D1])
        loop.at = sel_start
        l1_rows = loop.take([F, 3, F])
        fc_rows = loop.take([F, 7 * F])
        small_row = loop.take([1, 2 * F + 1])
        loop.at = key_w_start
        xt = loop.take([F, CH * P])
        loop.at = dsel_start
        y_rows = loop.take([P, YB, RELS * F])
        loop.at = acc_start
        rel_sb = loop.take([F, RELS, F])
        x0 = sb("x0", [P, CH, F])
        y_t = sb("y_t", [P, COLS + P - PC])
        body.restart()
        ring = body.take([P, CG, GB * SL])
        resident_start = body.at
        resident = body.take([P, RES * CG, GB * SL])
        cur = body.take([P, CH, F])
        kept = body.take([P, 4, CH, F])
        x3, u1, u2, u3 = [kept[:, k, :, :] for k in range(4)]
        ln_h, x1, ln_c = x0, u1, u3
        body.at = resident_start + CG * slice_bytes
        x1t = body.take([F, CH * P])
        body.at = resident_start
        feats = body.take([P, 2, CH, 2, F])
        feats_t = body.take([P, 2, 512])
        diffs = body.take([P, 2, CH, F])
        fc_out = body.take([P, CH, F])
        fc_neg = body.take([P, CH, F])
        fc_sum = body.take([P, CH, F])
        result = body.take([P, CH, F])
        ln_m = sb("ln_m", [P, 4, CH])
        ln_s = sb("ln_s", [P, 4, CH])
        ln_v = sb("ln_v", [P, 4, CH])
        ln_d = sb("ln_d", [P, 4, CH])
        ln_r = sb("ln_r", [P, 4, CH])
        deg = sb("deg", [P, CH])
        rdeg = sb("rdeg", [P, CH])

        ps = ctx.enter_context(nc.psum_tensor("ps", [P, 8, 512], F32))

        pads_set = sem("pads_set")
        main_loaded = [sem(f"loaded_{n}") for n in ("src", "dst", "typ", "w")]
        x_loaded = sem("x_loaded")
        x_zero = sem("x_zero")
        rel_loaded = sem("rel_loaded")
        w_loaded = sem("w_loaded")
        consts_made = sem("consts_made")
        consts_step = sem("consts_step")
        dve_step = sem("dve_step")
        xt_put = sem("xt_put")
        xt_copied = sem("xt_copied")
        y_put = sem("y_put")
        y_copied = sem("y_copied")
        y_stored = [sem(f"y_stored_{i}") for i in range(YB)]
        fc_step = sem("fc_step")
        small_put = sem("small_put")
        small_copied = sem("small_copied")
        edges_ready = sem("edges_ready")
        edges_put = sem("edges_put")
        edges_copied = sem("edges_copied")
        best_ready = sem("best_ready")
        best_put = sem("best_put")
        range_ready = sem("range_ready")
        range_put = sem("range_put")
        range_turned = sem("range_turned")
        range_stored = sem("range_stored")
        range_back = sem("range_back")
        tables_ready = sem("tables_ready")
        first_staged = sem("first_staged")
        staged = sem("staged")
        self_ready = sem("self_ready")
        sel_ready = sem("sel_ready")
        selb_ready = sem("selb_ready")
        keyw_ready = sem("keyw_ready")
        win_done = sem("win_done")
        win_out = sem("win_out")
        step_done = sem("step_done")
        blk_free = sem("blk_free")
        blk_stored = sem("blk_stored")
        xb_ready = sem("xb_ready")
        xs_ready = sem("xs_ready")
        x_done = sem("x_done")
        x_added = sem("x_added")
        ids_staged = sem("ids_staged")
        row_landed = [sem(f"row_landed_{s}") for s in range(TPC)]
        dst_staged = sem("dst_staged")
        dsel_ready = sem("dsel_ready")
        rel_done = sem("rel_done")
        rel_out = sem("rel_out")
        pe_through = sem("pe_through")
        pool_through = sem("pool_through")
        x_ids_staged = sem("x_ids_staged")
        x_row_landed = [sem(f"x_row_landed_{s}") for s in range(XC)]
        xd_ready = sem("xd_ready")
        xd_done = sem("xd_done")
        xd_added = sem("xd_added")
        landed = [sem(f"slice_landed_{s}") for s in range(CG)]
        resident_landed = [sem(f"resident_landed_{r}") for r in range(RES)]
        slice_used = sem("slice_used")
        x_ready = sem("x_ready")
        table_stored = sem("table_stored")
        y_end_set = sem("y_end_set")
        sum_copied = sem("sum_copied")
        cur_kept = sem("cur_kept")
        node_put = sem("node_put")
        own_put = sem("own_put")
        own_read = sem("own_read")
        own_added = sem("own_added")
        node_read = sem("node_read")
        x1t_put = sem("x1t_put")
        x1t_copied = sem("x1t_copied")
        deg_ready = sem("deg_ready")
        sq_in = sem("sq_in")
        sq_out = sem("sq_out")
        var_in = sem("var_in")
        sd_out = sem("sd_out")
        diff_ready = sem("diff_ready")
        feats_ready = sem("feats_ready")
        ft_put = sem("ft_put")
        ft_copied = sem("ft_copied")
        fc_put = sem("fc_put")
        out_ready = sem("out_ready")
        out_stored = sem("out_stored")
        sp_passed = sem("sp_passed")
        pe_passed = sem("pe_passed")
        pool_passed = sem("pool_passed")
        dve_passed = sem("dve_passed")

        EDGE_ARRAYS = [(gid_f, e_gid), (lo_f, e_all[:, :, 0]), (key_f, e_all[:, :, 1]), (w_f, e_all[:, :, 2]), (dst_f, e_dst)]
        FLAT = "p a b -> p (a b)"

        def edges_view(dram):
            a = FULL_G * P * P
            b = a + REST_T * P
            return (dram[0:a].rearrange("(h p e) -> p h e", p=P, e=P),
                    dram[a:b].rearrange("(p e) -> p e", e=P),
                    dram[b:E].rearrange("(p e) -> p e", p=1))

        KP = 6

        def general_tile(eng, lo, done, trip, size, width):
            return nc.s_assert_within(eng.snap(lo + done + trip * size), 0, TP - width, skip_runtime_bounds_check_because=
                                      "the trips end within one trip of the last real tile, which leaves room up to TP")

        def range_of(eng, table, n, most):
            return eng.value_load(table[0:1, bass.ds(n, 1)], min_val=0, max_val=most)

        block = ctx.enter_context(nc.Block())

        @block.sync
        def _(sp):
            sp.wait_ge(x_zero, 1)
            x_view = x_in.rearrange("(c p) f -> p c f", p=PC)
            for a, b in ((0, PC // 16 * 16), (PC // 16 * 16, PC)):
                sp.dma_start(x0[a:b, :, :], x_view[a:b, :, :]).then_inc(x_loaded, 16)
            sp.dma_start(rel_sb[:, :, :], rel_w.rearrange("r i o -> i r o")).then_inc(rel_loaded, 16)
            for n, (dram, tile) in enumerate([(src_in, src_i), (dst_in, dst_i), (type_in, typ_i), (weight_in, w_f)]):
                whole, tiles, rest = edges_view(dram)
                sp.dma_start(tile[:, 0:FULL_G, :], whole).then_inc(main_loaded[n], 16)
                if n == 0:
                    sp.wait_ge(pads_set, 4)
                sp.dma_start(tile[0:REST_T, FULL_G, :], tiles).then_inc(main_loaded[n], 16)
                sp.dma_start(tile[REST_T:REST_T + 1, FULL_G, 0:REST_E], rest).then_inc(main_loaded[n], 16)
            sp.dma_start(l1_rows[:, 0, :], l1_w[:, 0:F]).then_inc(w_loaded, 16)
            sp.dma_start(l1_rows[:, 1, :], l1_w[:, 0:F]).then_inc(w_loaded, 16)
            sp.dma_start(l1_rows[:, 2, :], l1_w[:, F:2 * F]).then_inc(w_loaded, 16)
            sp.dma_start(fc_rows[:, 0:F], fc_w[:, 0:F]).then_inc(w_loaded, 16)
            for at, first, n in ((1, 0, 2), (3, 4, 1), (4, 2, 1), (5, 5, 1), (6, 3, 1)):
                sp.dma_start(fc_rows[:, at * F:(at + n) * F], fc_w[:, first * F:(first + n) * F]).then_inc(w_loaded, 16)
            sp.dma_start(small_row[0:1, 0:F], l1_b.rearrange("(a n) -> a n", a=1)).then_inc(w_loaded, 16)
            sp.dma_start(small_row[0:1, F:2 * F], fc_b.rearrange("(a n) -> a n", a=1)).then_inc(w_loaded, 16)
            sp.dma_start(small_row[0:1, 2 * F:2 * F + 1], prelu_a.rearrange("(a n) -> a n", a=1)).then_inc(w_loaded, 16)
            sp.wait_ge(range_turned, 1)
            sp.dma_start(range_dram, range_t[:, :]).then_inc(range_stored, 16)
            sp.wait_ge(range_stored, 16)
            sp.dma_start(r_red[:, :, :], range_dram.rearrange("(o m b) p -> o m (b p)", o=1, m=2)).then_inc(range_back, 16)
            sp.sem_inc(blk_free, 2)
            views = [m[0].rearrange("g a p (b s) -> g b p a s", b=GB) for m in (weights_t, counts_t)]
            last_views = [m[1].rearrange("a p (b s) -> b p a s", b=LASTB) for m in (weights_t, counts_t)]

            def store(step, to):
                sp.wait_ge(win_out, WPS * step + WPS + 3)
                sp.sem_inc(sp_passed, 1)
                sp.wait_ge(step_done, step + 1)
                sp.sem_inc(sp_passed, 1)
                for m in range(2):
                    sp.dma_start(to[m], stage[:, bass.ds(step % 2, 1), m, :, :].rearrange("p o (a c) d -> p (o a) (c d)", a=CG)).then_inc(blk_stored, 16)
                sp.wait_ge(blk_stored, 32 * step + 32)
                sp.sem_inc(blk_free, 1)

            with sp.Fori(0, GROUPS - 1) as g:
                for b in range(GB):
                    store(g * GB + b, [view[g, b] for view in views])
            for b in range(LASTB):
                store((GROUPS - 1) * GB + b, [view[b] for view in last_views])

            def load(m, g, used):
                for cg in range(CG):
                    sp.wait_ge(slice_used, CG * used + cg + 1)
                    if isinstance(g, int) and g == GROUPS - 1:
                        sp.dma_start(ring[:, cg, 0:LASTB * SL], m[1][cg]).then_inc(landed[cg], 16)
                    else:
                        sp.dma_start(ring[:, cg, :], m[0][g, cg]).then_inc(landed[cg], 16)

            with sp.Fori(0, GROUPS - 1) as g:
                load(counts_t, g, g)
            load(counts_t, GROUPS - 1, GROUPS - 1)

            def keep(g):
                for cg in range(CG):
                    sp.dma_start(resident[:, CG * g + cg, :], weights_t[0][g, cg]).then_inc(resident_landed[g], 16)

            def load_product(k, resident_too):
                used = GROUPS * k
                for n, p in enumerate(STREAMED):
                    if resident_too and n < RES:
                        keep(n)
                    load(weights_t, ORDER[p], used)
                    used = GROUPS * k + p + 1

            sp.wait_ge(own_put, 1)
            load_product(1, True)
            with sp.Fori(2, KP) as k:
                load_product(k, False)
            sp.wait_ge(out_ready, 1)
            out_view = out.rearrange("(c p) f -> p c f", p=PC)
            for a, b in ((0, PC // 16 * 16), (PC // 16 * 16, PC)):
                sp.dma_start(out_view[a:b, :, :], result[a:b, :, :]).then_inc(out_stored, 16)
            sp.wait_ge(out_stored, 32)

        @block.gpsimd
        def _(pool):
            pool.memset(ident[:, :], 0.0).then_inc(consts_step, 1)
            pool.memset(ident2[:, :], 0.0).then_inc(consts_step, 1)
            pool.wait_ge(consts_step, 2)
            pool.affine_select(out=ident[:, :], in_=ident[:, :], compare_op=ALU.not_equal, fill=1.0, base=0,
                               pattern=[[-1, P]], channel_multiplier=1).then_inc(consts_made, 1)
            pool.affine_select(out=ident2[:, :], in_=ident2[:, :], compare_op=ALU.not_equal, fill=1.0, base=0,
                               pattern=[[-1, F]], channel_multiplier=1).then_inc(consts_step, 1)
            pool.wait_ge(consts_step, 3)
            pool.affine_select(out=ident2[:, :], in_=ident2[:, :], compare_op=ALU.not_equal, fill=1.0, base=-F,
                               pattern=[[-1, F]], channel_multiplier=1).then_inc(consts_made, 1)
            def narrow(a):
                return a[:, 0:WINS].rearrange("p (i j) -> p i j", j=WPS)[:, :, 0:NARROW]

            def wide(a):
                return a[:, 0:WINS].rearrange("p (i j) -> p i j", j=WPS)[:, :, NARROW:]

            ok = dict(allow_small_or_imprecise_dtypes=True)
            for out_, pattern, base, mul in (
                    (iota_b[:, :], [[1, 256]], 0, 0), (iota_f[:, :], [[1, P]], 0, 0), (narrow(win_base), [[PC * CH, STEPS], [(WIN - 1) * CH, NARROW]], 0, 0),
                    (wide(win_base), [[PC * CH, STEPS], [WC, WPS - NARROW]], START[NARROW] * CH, 0),
                    (narrow(first_dst), [[PC, STEPS], [WIN - 1, NARROW]], 0, 0), (narrow(last_dst), [[PC, STEPS], [WIN - 1, NARROW]], WIN - 2, 0),
                    (wide(first_dst), [[PC, STEPS], [WIN, WPS - NARROW]], START[NARROW], 0),
                    (wide(last_dst), [[PC, STEPS], [WIN, WPS - NARROW]], START[NARROW] + WIN - 1, 0),
                    (first_dst[:, WINS:RC], [[PC, RC - WINS]], 0, 0), (last_dst[:, WINS:RC], [[PC, RC - WINS]], PC - 1, 0),
                    (chunk_base[:, :], [[PC, STEPS]], 0, 0), (tile_no[:, :], [[P, TG]], 1, 1), (tile_left[:, :], [[-P, TG]], TP, -1)):
                pool.iota(out_, pattern, base=base, channel_multiplier=mul, **ok).then_inc(consts_made, 1)
            pool.memset(x_gathered[:, :, :], 1.0).then_inc(consts_step, 1)
            pool.memset(gathered[:, :, :], 1.0).then_inc(consts_step, 1)
            pool.memset(acc2[:, 0, :], 0.0).then_inc(consts_step, 1)
            pool.memset(acc2[:, 1:1 + CH, F:F + 1], 0.0).then_inc(consts_step, 1)
            pool.wait_ge(x_loaded, 32)
            pool.tensor_copy(acc2[:, 1:1 + CH, 0:F], x0[:, :, :]).then_inc(consts_step, 1)
            pool.memset(ones_row[:, :], 1.0).then_inc(consts_made, 1)
            pool.wait_ge(consts_step, 8)
            pool.wait_ge(tables_ready, 1)
            for b in range(YB):
                pool.wait_ge(y_stored[b], 16 * ((CH + YB - 1 - b) // YB))
            pool.sem_inc(table_stored, 1)
            with pool.Fori(0, STEPS) as i:
                lo = range_of(pool, tab_lo, WINS + i, TP - TPC)
                parts = [(a, min(a + GG, TPC)) for a in range(0, TPC, GG)]

                def stage_ids(g):
                    a, b = parts[g]
                    pool.wait_ge(rel_done, TPC * i + b)
                    pool.tensor_copy(gid_stage[:, a:b], e_gid[:, bass.ds(lo + a, b - a)]).then_inc(ids_staged, 1)

                stage_ids(0)
                for g, (a, b) in enumerate(parts):
                    if g + 1 < len(parts):
                        stage_ids(g + 1)
                    pool.wait_ge(ids_staged, len(parts) * i + g + 1)
                    pool.sem_inc(pool_passed, 1)
                    for s in range(a, b):
                        pool.indirect_dma_start(
                            out=gathered[:, s, 0:F], out_offset=None, in_=y_dram[:, :],
                            in_offset=bass.IndirectOffsetOnAxis(ap=gid_stage[:, s:s + 1], axis=0)).then_inc(row_landed[s], 16)
                ex = range_of(pool, tab_ex, WINS + i, TP // XC)
                with pool.If(ex > 0):
                    cum = range_of(pool, tab_cum, WINS + i, STEPS * TP // XC)
                    with pool.Fori(0, ex) as trip:
                        pool.wait_ge(xd_done, cum + trip + 1)
                        pool.tensor_copy(x_gid_stage[:, :], e_gid[:, bass.ds(general_tile(pool, lo, TPC, trip, XC, XC), XC)]).then_inc(x_ids_staged, 1)
                        pool.wait_ge(x_ids_staged, cum + trip + 1)
                        pool.sem_inc(pool_passed, 1)
                        for q in range(XC):
                            pool.indirect_dma_start(
                                out=x_gathered[:, q, 0:F], out_offset=None, in_=y_dram[:, :],
                                in_offset=bass.IndirectOffsetOnAxis(ap=x_gid_stage[:, q:q + 1], axis=0)).then_inc(x_row_landed[q], 16)
                pool.sem_inc(pool_passed, 1)
            pool.sem_inc(pool_through, 1)

        @block.scalar
        def _(act):
            for q in range(-(-CH // 4)):
                n = min(4, CH - 4 * q) * P
                act.wait_ge(xt_put, q + 1)
                act.copy(xt[:, 512 * q:512 * q + n], ps[0:F, 4 + q % 2, 0:n]).then_inc(xt_copied, 1)
            u = 0
            for _, e_arr in EDGE_ARRAYS:
                for h in range(0, TG, 4):
                    n = min(4, TG - h) * P
                    act.wait_ge(edges_put, u + 1)
                    act.copy(e_arr[:, P * h:P * h + n], ps[:, 4 + u % 2, 0:n]).then_inc(edges_copied, 1)
                    u += 1
            for c in range(CH):
                act.wait_ge(y_put, c + 1)
                if c >= YB:
                    act.wait_ge(y_stored[c % YB], 16 * (c // YB))
                act.copy(y_rows[:, c % YB, :].rearrange("p (b n) -> p b n", b=2), ps[:, 2 * (c % 2):2 * (c % 2) + 2, :]).then_inc(y_copied, 1)
                act.wait_ge(y_copied, c + 1)
                act.dma_start(y_dram.rearrange("(c p r) f -> c p (r f)", p=P, r=RELS)[c], y_rows[:, c % YB, :]).then_inc(y_stored[c % YB], 16)
            act.wait_ge(tables_ready, 1)
            act.sem_inc(win_out, 3)
            act.sem_inc(keyw_ready, 1)
            act.sem_inc(staged, WPS - 1)

            def stage_window(n, slot):
                lo = range_of(act, tab_lo, n, TP - TPC)
                act.copy(e_stage[:, slot, :].rearrange("p (t k) -> p t k", k=3), e_all[:, bass.ds(lo, TPW), :]).then_inc(staged, 1)

            def put_out(n, j, turn):
                act.wait_ge(win_done, n + 4)
                d = START[j + 1] - START[j]
                act.copy(stage[:, bass.ds(turn, 1), :, :, START[j]:START[j + 1]].rearrange("p o m c d -> p (o m c) d"),
                         ps[:, SLOT[j], 0:2 * WC].rearrange("p (m d c) -> p m c d", m=2, c=CH)[:, :, :, 0:d]).then_inc(win_out, 1)

            with act.Fori(0, STEPS) as i:
                turn = act.snap(i % 2)
                for j in range(WPS):
                    n = WPS * i + j
                    act.wait_ge(sel_ready, n + 1)
                    for s in range(TPW):
                        last = act.activation(key_w[:, SLOT[j], s, :], key_b[:, SLOT[j], s, 0:WC], ACT.Copy, scale=e_stage[:, j, 3 * s + 2:3 * s + 3])
                    last.then_inc(keyw_ready, 1)
                    act.wait_ge(keyw_ready, n + 1)
                    stage_window(n + WPS - 1, j - 1 if j else WPS - 1)
                    if j == 1:
                        act.wait_ge(blk_free, i + 1)
                    if j:
                        put_out(n - 1, j - 1, turn)
                put_out(WPS * i + WPS - 1, WPS - 1, turn)

            def sums(gg, p, g, width=GN):
                act.wait_ge(slice_used, CG * (gg + 1) + CG)
                act.copy(y_t[:, bass.ds(g * GN, width)], ps[:, BANK[p], 0:width]).then_inc(sum_copied, 1)

            def product(k):
                act.wait_ge(node_put, k)
                for p, g in enumerate(ORDER):
                    sums(GROUPS * k + p, p, g, LASTB * BLK if g == GROUPS - 1 else GN)

            def norm(n, squares):
                for i, (a, b) in enumerate(HALVES):
                    act.wait_ge(sq_in, 2 * n + i + 1)
                    act.activation(squares[:, a:b, :], ln_c[:, a:b, :], ACT.Square).then_inc(sq_out, 1)
                act.wait_ge(var_in, n + 1)
                act.activation(ln_d[:, n, :], ln_v[:, n, :], ACT.Sqrt).then_inc(sd_out, 1)

            norm(0, x1)
            act.wait_ge(x_ready, 1)
            act.sem_inc(sum_copied, 2)
            for q in range(-(-CH // 4)):
                n = min(4, CH - 4 * q) * P
                act.wait_ge(x1t_put, q + 1)
                act.copy(x1t[:, 512 * q:512 * q + n], ps[0:F, 4 + q % 2, 0:n]).then_inc(x1t_copied, 1)
            with act.Fori(0, (GROUPS - 1) // 2) as it:
                for p in range(2):
                    sums(2 * it + p, p, 2 * it + p)
            sums(GROUPS - 1, GROUPS - 1, GROUPS - 1, LASTB * BLK)
            norm(1, cur)
            product(1)
            norm(2, cur)
            with act.Fori(2, KP) as k:
                act.wait_ge(x_ready, k + 1)
                act.copy(kept[:, bass.ds(k - 2, 1), :, :].rearrange("p o c f -> p (o c f)"), cur[:, :, :].rearrange(FLAT)).then_inc(cur_kept, 1)
                product(k)
            for u in range(14):
                n = min(4, CH - 4 * (u % 7)) * P
                act.wait_ge(ft_put, u + 1)
                if u >= 2:
                    act.wait_ge(fc_put, u - 1)
                act.copy(feats_t[:, u % 2, 0:n], ps[:, 2 + u % 2, 0:n]).then_inc(ft_copied, 1)
            norm(3, fc_sum)

        @block.vector
        def _(v):
            steps = [0]

            def link(ins):
                steps[0] += 1
                ins.then_inc(dve_step, 1)
                v.wait_ge(dve_step, steps[0])

            v.memset(x0[:, :, :], 0.0).then_inc(x_zero, 1)
            v.memset(y_t[:, COLS:COLS + P - PC], 0.0).then_inc(y_end_set, 1)
            v.memset(dst_i[:, FULL_G, :], -1).then_inc(pads_set, 1)
            v.memset(src_i[:, FULL_G, :], 0).then_inc(pads_set, 1)
            v.memset(typ_i[:, FULL_G, :], 0).then_inc(pads_set, 1)
            v.memset(w_f[:, FULL_G, :], 0.0).then_inc(pads_set, 1)
            v.wait_ge(consts_made, 16)
            for n in range(4):
                v.wait_ge(main_loaded[n], 48)
            link(v.tensor_scalar(tmp_i[:, :, :], src_i[:, :, :], float(DIV_MUL), None, ALU.mult))
            link(v.tensor_scalar(tmp2_i[:, :, :], tmp_i[:, :, :], DIV_SHIFT, None, ALU.arith_shift_right))
            v.tensor_copy(hi_f[:, :, :], tmp2_i[:, :, :])
            v.tensor_copy(src_f[:, :, :], src_i[:, :, :])
            v.tensor_copy(scr_f[:, :, :], typ_i[:, :, :])
            link(v.tensor_copy(dst_f[:, :, :], dst_i[:, :, :]))
            v.scalar_tensor_tensor(out=lo_f[:, :, :], in0=hi_f[:, :, :], scalar=-float(PC), in1=src_f[:, :, :], op0=ALU.mult, op1=ALU.add)
            link(v.scalar_tensor_tensor(out=scr2_f[:, :, :], in0=hi_f[:, :, :], scalar=float(P - PC), in1=src_f[:, :, :], op0=ALU.mult, op1=ALU.add))
            v.scalar_tensor_tensor(out=gid_f[:, :, :], in0=scr2_f[:, :, :], scalar=float(RELS), in1=scr_f[:, :, :], op0=ALU.mult, op1=ALU.add)
            link(v.scalar_tensor_tensor(out=key_f[:, :, :], in0=dst_f[:, :, :], scalar=float(CH), in1=hi_f[:, :, :], op0=ALU.mult, op1=ALU.add))
            v.sem_inc(edges_ready, 1)
            v.tensor_reduce(t_max[:, :], dst_f[:, :, :], axis=AX.X, op=ALU.max)
            link(v.tensor_scalar(scr2_f[:, :, :], dst_f[:, :, :], 0.0, 5000.0, ALU.is_lt, ALU.mult))
            link(v.tensor_tensor(scr_f[:, :, :], scr2_f[:, :, :], dst_f[:, :, :], ALU.add))
            v.tensor_reduce(t_min[:, :], scr_f[:, :, :], axis=AX.X, op=ALU.min)
            v.memset(r_zero[:, :], 0.0)
            link(v.memset(best[:, :, 0, :], 0.0))
            for h in range(TG):
                last = v.tensor_scalar(has_a[:, h, :], last_dst[:, :], t_min[:, h:h + 1], None, ALU.is_ge)
            link(last)
            for h in range(TG):
                last = v.scalar_tensor_tensor(out=has[:, h, :], in0=first_dst[:, :], scalar=t_max[:, h:h + 1], in1=has_a[:, h, :], op0=ALU.is_le, op1=ALU.mult)
            link(last)
            for h in range(TG):
                a, b = h % 2, (h + 1) % 2
                v.scalar_tensor_tensor(out=best[:, 0, b, :], in0=has[:, h, :], scalar=tile_left[:, h:h + 1], in1=best[:, 0, a, :], op0=ALU.mult, op1=ALU.max)
                link(v.scalar_tensor_tensor(out=best[:, 1, b, :], in0=has[:, h, :], scalar=tile_no[:, h:h + 1], in1=best[:, 1, a, :], op0=ALU.mult, op1=ALU.max))
            v.sem_inc(best_ready, 1)
            v.wait_ge(small_put, 1)
            v.tensor_copy(wa2_t[:, :], ps[:, 6, 0:F])
            v.tensor_copy(wb_t[:, :], ps[0:F, 6, F:2 * F])
            v.tensor_copy(fc_t[:, :, :], ps[:, 6, 128:128 + 3 * F].rearrange("p (j f) -> p j f", f=F)).then_inc(fc_step, 1)
            v.wait_ge(fc_step, 1)
            v.tensor_tensor(fc_t[0:F, 1, :], fc_t[0:F, 1, :], ps[0:F, 6, 128 + 3 * F:128 + 4 * F], ALU.add).then_inc(fc_step, 1)
            v.tensor_copy(small[:, :], ps[:, 7, 0:2 * F + 1]).then_inc(small_copied, 1)
            v.wait_ge(best_put, 1)
            v.tensor_reduce(range_red[:, :, :], ps[:, 6:8, 0:RC].rearrange("p m (b t) -> p m b t", t=P), axis=AX.X, op=ALU.max).then_inc(range_ready, 1)
            v.wait_ge(range_put, 1)
            v.tensor_copy(range_t[:, :], ps[0:6, 6, 0:P]).then_inc(range_turned, 1)
            v.wait_ge(range_back, 16)
            link(v.tensor_scalar(r_a[:, :], r_red[:, 0, :], -1.0, float(TP), ALU.mult, ALU.add))
            link(v.tensor_scalar(r_lo[:, :], r_a[:, :], float(TP - TPC), None, ALU.min))
            v.tensor_copy(tab_lo[:, :], r_lo[:, :])
            link(v.tensor_tensor(r_k[:, :], r_red[:, 1, :], r_lo[:, :], ALU.subtract))
            for a, b, done, trip in ((0, WINS, TPW, XT), (WINS, RC, TPC, XC)):
                link(v.tensor_scalar(r_a[:, a:b], r_k[:, a:b], -float(done), 0.0, ALU.add, ALU.max))
                link(v.tensor_scalar(r_k[:, a:b], r_a[:, a:b], float(trip - 1), None, ALU.add))
                link(v.tensor_copy(r_ki[:, a:b], r_k[:, a:b]))
                link(v.tensor_scalar(tab_ex[:, a:b], r_ki[:, a:b], trip.bit_length() - 1, None, ALU.arith_shift_right))
                link(v.tensor_copy(r_ex[:, a:b], tab_ex[:, a:b]))
                link(v.tensor_tensor_scan(r_cum[:, a:b], r_ex[:, a:b], r_zero[:, a:b], 0.0, ALU.add, ALU.add))
                link(v.tensor_tensor(r_a[:, a:b], r_cum[:, a:b], r_ex[:, a:b], ALU.subtract))
            v.tensor_copy(tab_cum[:, :], r_a[:, :])
            v.tensor_reduce(tab_win[:, :], r_ex[:, 0:WINS].rearrange("o (i j) -> o i j", j=WPS), axis=AX.X, op=ALU.max)
            link(v.tensor_reduce(r_k[:, 0:STEPS], r_ex[:, 0:WINS].rearrange("o (i j) -> o i j", j=WPS), axis=AX.X, op=ALU.max))
            v.tensor_tensor(tab_any[:, :], r_k[:, 0:STEPS], r_ex[:, WINS:WINS + STEPS], ALU.max).then_inc(tables_ready, 1)
            v.wait_ge(tables_ready, 1)

            v.sem_inc(dsel_ready, DB)
            for n in range(WPS - 1):
                lo = range_of(v, tab_lo, n, TP - TPC)
                v.tensor_copy(e_stage[:, n, :].rearrange("p (t k) -> p t k", k=3), e_all[:, bass.ds(lo, TPW), :]).then_inc(first_staged, 1)
            v.wait_ge(first_staged, WPS - 1)

            def window_slow(i, j, turn, start, d):
                n = v.snap(WPS * i + j)
                ex = range_of(v, tab_ex, n, TP // XT)
                with v.If(ex > 0):
                    cum = range_of(v, tab_cum, n, WINS * TP // XT)
                    lo = range_of(v, tab_lo, n, TP - TPC)
                    with v.Fori(0, ex) as trip:
                        t = general_tile(v, lo, TPW, trip, XT, XT)
                        for q in range(XT):
                            v.tensor_scalar(x_key_b[:, q, :], iota_b[:, 0:WS], win_base[:, bass.ds(n, 1)], e_all[:, bass.ds(t + q, 1), 1], ALU.add, ALU.is_equal)
                            v.tensor_scalar(x_sel_b[:, q, :], iota_b[:, 0:P], e_all[:, bass.ds(t + q, 1), 0], None, ALU.is_equal)
                            last = v.tensor_scalar(x_sel_f[:, q, :], iota_f[:, :], e_all[:, bass.ds(t + q, 1), 0], None, ALU.is_equal)
                        last.then_inc(xb_ready, 1)
                        v.wait_ge(xb_ready, cum + trip + 1)
                        for q in range(XT):
                            last = v.tensor_scalar(x_key_w[:, q, :], x_key_b[:, q, :], e_all[:, bass.ds(t + q, 1), 2], None, ALU.mult)
                        last.then_inc(xs_ready, 1)
                        v.wait_ge(x_done, cum + trip + 1)
                        for m in range(2):
                            a = stage[:, bass.ds(turn, 1), m, :, bass.ds(start, d)].rearrange("p o c d -> p (o c) d")
                            last = v.tensor_tensor(a, a, ps[:, 7, WS * m:WS * m + WC].rearrange("p (d c) -> p c d", c=CH)[:, :, 0:d], ALU.add)
                        last.then_inc(x_added, 1)
                        v.wait_ge(x_added, cum + trip + 1)
                        v.sem_inc(dve_passed, 1)
                v.sem_inc(dve_passed, 1)

            with v.Fori(0, STEPS) as i:
                lo = range_of(v, tab_lo, WINS + i, TP - TPC)
                v.wait_ge(dsel_ready, DB * i + DB)
                v.tensor_scalar(dst_stage[:, :], e_dst[:, bass.ds(lo, TPC)], chunk_base[:, bass.ds(i, 1)], None, ALU.subtract).then_inc(dst_staged, 1)
                for j in range(WPS):
                    n = WPS * i + j
                    base = win_base[:, bass.ds(n, 1)]
                    if j == WPS - 1:
                        some = range_of(v, tab_any, i, TP // XC)
                    v.wait_ge(staged, n + 1)
                    v.wait_ge(win_done, n + 1)
                    v.tensor_tensor(sel_f[:, SLOT[j], :, :], iota_f[:, :].unsqueeze(1).to_broadcast([P, TPW, P]),
                                    e_stage[:, j, 0:3 * TPW:3].unsqueeze(2).to_broadcast([P, TPW, P]), ALU.is_equal).then_inc(self_ready, 1)
                    for s in range(TPW):
                        last = v.tensor_scalar(key_b[:, SLOT[j], s, :], iota_b[:, 0:WS], base, e_stage[:, j, 3 * s + 1:3 * s + 2], ALU.add, ALU.is_equal)
                    last.then_inc(sel_ready, 1)
                    v.wait_ge(self_ready, n + 1)
                    v.tensor_copy(sel_b[:, SLOT[j], :, :], sel_f[:, SLOT[j], :, :]).then_inc(selb_ready, 1)
                    if j == 1:
                        v.wait_ge(table_stored, 1)
                        v.wait_ge(rel_done, TPC * i + TPC)
                        v.tensor_tensor(acc[:, bass.ds(i, 1), :].rearrange(FLAT), ps[:, 6, 0:D1], acc2[:, bass.ds(i, 1), :].rearrange(FLAT), ALU.add).then_inc(rel_out, 1)
                        v.wait_ge(dst_staged, i + 1)
                    if AFTER[j]:
                        a, b = AFTER[j][0], AFTER[j][-1] + 1
                        v.wait_ge(rel_done, TPC * i + b)
                        v.tensor_tensor(dsel[:, a:b, :], iota_f[:, :].unsqueeze(1).to_broadcast([P, b - a, P]),
                                        dst_stage[:, a:b].unsqueeze(2).to_broadcast([P, b - a, P]), ALU.is_equal).then_inc(dsel_ready, 1)
                with v.If(some > 0):
                    v.wait_ge(win_out, WPS * i + WPS + 3)
                    v.sem_inc(dve_passed, 1)
                    windows = range_of(v, tab_win, i, TP // XT)
                    turn = v.snap(i % 2)
                    with v.If(windows > 0):
                        with v.Fori(0, NARROW) as j:
                            window_slow(i, j, turn, (WIN - 1) * j, WIN - 1)
                        with v.Fori(NARROW, WPS) as j:
                            window_slow(i, j, turn, WIN * j - NARROW, WIN)
                    v.sem_inc(dve_passed, 1)
                    ex = range_of(v, tab_ex, WINS + i, TP // XC)
                    with v.If(ex > 0):
                        cum = range_of(v, tab_cum, WINS + i, STEPS * TP // XC)
                        with v.Fori(0, ex) as trip:
                            t = general_tile(v, lo, TPC, trip, XC, XC)
                            for q in range(XC):
                                last = v.tensor_scalar(x_dsel[:, q, :], iota_f[:, :], chunk_base[:, bass.ds(i, 1)], e_dst[:, bass.ds(t + q, 1)], ALU.add, ALU.is_equal)
                            last.then_inc(xd_ready, 1)
                            v.wait_ge(xd_done, cum + trip + 2)
                            a = acc2[:, bass.ds(i + 1, 1), :].rearrange(FLAT)
                            v.tensor_tensor(a, a, ps[:, 7, 0:D1], ALU.add).then_inc(xd_added, 1)
                            v.wait_ge(xd_added, cum + trip + 1)
                            v.sem_inc(dve_passed, 1)
                    v.sem_inc(dve_passed, 1)
                v.sem_inc(step_done, 1)
            v.wait_ge(rel_done, TPC * STEPS + TPC)
            link(v.tensor_tensor(acc[:, STEPS, :], ps[:, 6, 0:D1], acc2[:, STEPS, :], ALU.add))
            v.wait_ge(win_out, WINS + 3)
            v.wait_ge(win_done, WINS + 3)
            v.wait_ge(pe_through, 1)
            v.wait_ge(pool_through, 1)

            def bcast(m):
                return m.unsqueeze(2).to_broadcast([P, CH, F])

            def norm(n, h, squares, x_out):
                link(v.tensor_reduce(ln_s[:, n, :], h, axis=AX.X, op=ALU.add))
                link(v.tensor_scalar(ln_m[:, n, :], ln_s[:, n, :], 1.0 / F, None, ALU.mult))
                for a, b in HALVES:
                    v.tensor_tensor(ln_c[:, a:b, :], h[:, a:b, :], ln_m[:, n, a:b].unsqueeze(2).to_broadcast([P, b - a, F]), ALU.subtract).then_inc(sq_in, 1)
                for i, (a, b) in enumerate(HALVES):
                    v.wait_ge(sq_out, 2 * n + i + 1)
                    last = v.tensor_reduce(ln_s[:, n, a:b], squares[:, a:b, :], axis=AX.X, op=ALU.add)
                link(last)
                v.tensor_scalar(ln_v[:, n, :], ln_s[:, n, :], 1.0 / F, EPS, ALU.mult, ALU.add).then_inc(var_in, 1)
                v.wait_ge(sd_out, n + 1)
                link(v.reciprocal(ln_r[:, n, :], ln_d[:, n, :]))
                return v.tensor_tensor(x_out[:, :, :], ln_c[:, :, :], bcast(ln_r[:, n, :]), ALU.mult)

            node_sums = ps[:, 2:6, :].rearrange("p b n -> p (b n)")[:, 0:CH * F].rearrange("p (c f) -> p c f", f=F)
            v.tensor_scalar(deg[:, :], acc[:, 1:1 + CH, F], 1.0, None, ALU.max).then_inc(deg_ready, 1)
            v.wait_ge(deg_ready, 1)
            v.reciprocal(rdeg[:, :], deg[:, :])
            norm(0, acc[:, 1:1 + CH, 0:F], x1, x1).then_inc(x_ready, 1)
            v.wait_ge(own_put, 1)
            v.wait_ge(x_ready, 1)
            for i, b in enumerate((6, 7, 4, 5)):
                n = min(8, CH - 8 * i)
                last = v.tensor_tensor(ln_c[:, 8 * i:8 * i + n, :], ps[:, b, :].rearrange("p (c f) -> p c f", f=F)[:, 0:n, :], x1[:, 8 * i:8 * i + n, :], ALU.add)
            last.then_inc(own_read, 1)
            v.wait_ge(own_read, 1)
            v.tensor_tensor(cur[:, :, :], ln_c[:, :, :], small[:, 0:F].unsqueeze(1).to_broadcast([P, CH, F]), ALU.add).then_inc(own_added, 1)
            v.wait_ge(own_added, 1)
            v.wait_ge(node_put, 1)
            link(v.tensor_tensor(ln_h[:, :, :], node_sums, bcast(rdeg[:, :]), ALU.mult))
            link(v.tensor_tensor(ln_h[:, :, :], ln_h[:, :, :], cur[:, :, :], ALU.add))
            norm(1, ln_h[:, :, :], cur, cur).then_inc(x_ready, 1)
            v.wait_ge(node_put, 2)
            v.wait_ge(x_ready, 2)
            v.tensor_tensor(ln_h[:, :, :], node_sums, cur[:, :, :], ALU.add).then_inc(node_read, 1)
            v.wait_ge(node_read, 1)
            norm(2, ln_h[:, :, :], cur, cur).then_inc(x_ready, 1)
            def pair(j, parts):
                for i, (a, b) in enumerate(parts):
                    v.tensor_tensor(diffs[:, i, :, :], a[:, :, :], b[:, :, :], ALU.subtract).then_inc(diff_ready, 1)
                for i in range(2):
                    v.wait_ge(diff_ready, 2 * j + i + 1)
                    v.scalar_tensor_tensor(out=feats[:, j, :, i, :], in0=diffs[:, i, :, :], scalar=-1.0, in1=diffs[:, i, :, :], op0=ALU.mult, op1=ALU.max).then_inc(feats_ready, 1)

            for k in range(2, KP):
                v.wait_ge(slice_used, CG * GROUPS * (k + 1) + CG)
                v.wait_ge(cur_kept, k - 1)
                if k == 2:
                    v.wait_ge(x_ready, 3)
                v.tensor_copy(cur[:, 0:FIRST, :], node_sums[:, 0:FIRST, :])
                v.wait_ge(node_put, k + 1)
                v.tensor_copy(cur[:, FIRST:, :], node_sums[:, FIRST:, :]).then_inc(x_ready, 1)
            v.wait_ge(x_ready, 7)
            u4 = cur
            pair(0, ((u1, u2), (u3, u2)))
            v.wait_ge(feats_ready, 2)
            pair(1, ((u2, u4), (u4, u3)))
            v.wait_ge(fc_put, 14)
            v.wait_ge(feats_ready, 4)
            fc_sums = [ps[:, b, :].rearrange("p (c f) -> p c f", f=F) for b in (0, 1, 6, 7)]
            for i, b in enumerate(fc_sums):
                n = min(8, CH - 8 * i)
                last = v.tensor_tensor(fc_out[:, 8 * i:8 * i + n, :], b[:, 0:n, :], small[:, F:2 * F].unsqueeze(1).to_broadcast([P, n, F]), ALU.add)
            link(last)
            v.tensor_scalar(fc_neg[:, :, :], fc_out[:, :, :], 0.0, small[:, 2 * F:2 * F + 1], ALU.min, ALU.mult)
            link(v.scalar_tensor_tensor(out=fc_sum[:, :, :], in0=fc_out[:, :, :], scalar=0.0, in1=x3[:, :, :], op0=ALU.max, op1=ALU.add))
            link(v.tensor_tensor(ln_h[:, :, :], fc_sum[:, :, :], fc_neg[:, :, :], ALU.add))
            norm(3, ln_h[:, :, :], fc_sum, result).then_inc(out_ready, 1)

        @block.tensor
        def _(pe):
            def transposed(x, put, copied):
                for q in range(-(-CH // 4)):
                    if q >= 2:
                        pe.wait_ge(copied, q - 1)
                    for c in range(4 * q, min(4 * q + 4, CH)):
                        last = pe.transpose(ps[0:F, 4 + q % 2, P * (c % 4):P * (c % 4) + P], x[:, c, :], ident[:, :])
                    last.then_inc(put, 1)

            pe.wait_ge(consts_made, 16)
            pe.wait_ge(x_loaded, 32)
            transposed(x0, xt_put, xt_copied)
            pe.wait_ge(edges_ready, 1)
            u = 0
            for f_arr, _ in EDGE_ARRAYS:
                for h in range(0, TG, 4):
                    if u >= 2:
                        pe.wait_ge(edges_copied, u - 1)
                    elif u == 0:
                        pe.wait_ge(xt_copied, -(-CH // 4))
                    for g in range(h, min(h + 4, TG)):
                        last = pe.transpose(ps[:, 4 + u % 2, P * (g - h):P * (g - h) + P], f_arr[:, g, :], ident[:, :])
                    last.then_inc(edges_put, 1)
                    u += 1
            pe.wait_ge(w_loaded, 16 * 12)
            pe.transpose(ps[:, 6, 0:F], l1_rows[:, 0:2, :].rearrange(FLAT), ident[0:F, 0:F])
            pe.transpose(ps[0:F, 6, F:2 * F], l1_rows[:, 2, :], ident[0:F, 0:F])
            for j in range(3):
                pe.transpose(ps[:, 6, 128 + F * j:128 + F * j + F], fc_rows[:, P * j:P * j + P], ident[0:F, 0:F])
            pe.transpose(ps[0:F, 6, 128 + 3 * F:128 + 4 * F], fc_rows[:, 6 * F:7 * F], ident[0:F, 0:F])
            pe.matmul(ps[:, 7, 0:2 * F + 1], ones_row[:, :], small_row[:, :], start=True, stop=True).then_inc(small_put, 1)

            def ranges():
                pe.wait_ge(best_ready, 1)
                pe.wait_ge(small_copied, 1)
                for m in range(2):
                    for b in range(3):
                        last = pe.transpose(ps[:, 6 + m, P * b:P * b + P], best[:, m, TG % 2, P * b:P * b + P], ident[:, :])
                last.then_inc(best_put, 1)
                pe.wait_ge(range_ready, 1)
                pe.transpose(ps[0:6, 6, 0:P], range_red[:, :, :].rearrange(FLAT), ident[:, :]).then_inc(range_put, 1)

            pe.wait_ge(rel_loaded, 16)
            for c in range(CH):
                if c == 8:
                    ranges()
                pe.wait_ge(xt_copied, c // 4 + 1)
                if c >= 2:
                    pe.wait_ge(y_copied, c - 1)
                for i in range(2):
                    last = pe.matmul(ps[:, 2 * (c % 2) + i, :], xt[:, c * P:c * P + P], rel_sb[:, 8 * i:8 * i + 8, :].rearrange("i r o -> i (r o)"), start=True, stop=True)
                last.then_inc(y_put, 1)
            pe.wait_ge(tables_ready, 1)
            pe.sem_inc(win_done, 3)
            pe.sem_inc(rel_done, TPC)
            pe.sem_inc(xd_done, 1)
            with pe.Fori(0, STEPS) as i:
                for j in range(WPS):
                    n = WPS * i + j
                    if j == WPS - 1:
                        some = range_of(pe, tab_any, i, TP // XC)
                    pe.wait_ge(selb_ready, n + 1)
                    pe.wait_ge(keyw_ready, n + 2)
                    pe.wait_ge(win_out, n + 1)
                    for s in range(TPW):
                        pe.matmul(ps[:, SLOT[j], 0:WC], sel_f[:, SLOT[j], s, :], key_w[:, SLOT[j], s, :], start=(s == 0), stop=(s == TPW - 1))
                    for s in range(TPW):
                        last = pe.matmul(ps[:, SLOT[j], WC:2 * WC], sel_b[:, SLOT[j], s, :], key_b[:, SLOT[j], s, 0:WC], start=(s == 0), stop=(s == TPW - 1))
                    last.then_inc(win_done, 1)
                    if AFTER[j]:
                        pe.wait_ge(dsel_ready, DB * i + DB + j - 1)
                    for s in AFTER[j]:
                        pe.wait_ge(row_landed[s], 16 * i + 16)
                        if s == 0:
                            pe.wait_ge(rel_out, i + 1)
                        pe.matmul(ps[:, 6, 0:D1], dsel[:, s, :], gathered[:, s, :], start=(s == 0), stop=(s == TPC - 1)).then_inc(rel_done, 1)
                with pe.If(some > 0):
                    windows = range_of(pe, tab_win, i, TP // XT)
                    with pe.If(windows > 0):
                        with pe.Fori(0, WPS) as j:
                            n = pe.snap(WPS * i + j)
                            ex = range_of(pe, tab_ex, n, TP // XT)
                            with pe.If(ex > 0):
                                cum = range_of(pe, tab_cum, n, WINS * TP // XT)
                                with pe.Fori(0, ex) as trip:
                                    pe.wait_ge(xs_ready, cum + trip + 1)
                                    for q in range(XT):
                                        pe.matmul(ps[:, 7, 0:WC], x_sel_f[:, q, :], x_key_w[:, q, 0:WC], start=(q == 0), stop=(q == XT - 1))
                                    for q in range(XT):
                                        last = pe.matmul(ps[:, 7, WS:WS + WC], x_sel_b[:, q, :], x_key_b[:, q, 0:WC], start=(q == 0), stop=(q == XT - 1))
                                    last.then_inc(x_done, 1)
                            pe.sem_inc(pe_passed, 1)
                    pe.sem_inc(pe_passed, 1)
                    ex = range_of(pe, tab_ex, WINS + i, TP // XC)
                    with pe.If(ex > 0):
                        cum = range_of(pe, tab_cum, WINS + i, STEPS * TP // XC)
                        with pe.Fori(0, ex) as trip:
                            pe.wait_ge(xd_ready, cum + trip + 1)
                            for q in range(XC):
                                pe.wait_ge(x_row_landed[q], (cum + trip) * 16 + 16)
                                last = pe.matmul(ps[:, 7, 0:D1], x_dsel[:, q, :], x_gathered[:, q, :], start=(q == 0), stop=(q == XC - 1))
                            last.then_inc(xd_done, 1)
                    pe.sem_inc(pe_passed, 1)
                pe.sem_inc(pe_passed, 1)
            pe.sem_inc(pe_through, 1)

            pe.wait_ge(x_ready, 1)
            transposed(x1, x1t_put, x1t_copied)
            pe.wait_ge(x1t_copied, -(-CH // 4))
            for c in range(CH):
                last = pe.matmul(ps[:, (6, 7, 4, 5)[c // 8], F * (c % 8):F * (c % 8) + F], x1t[:, c * P:c * P + P], wb_t[:, :], start=True, stop=True)
            last.then_inc(own_put, 1)
            pe.sem_inc(slice_used, CG)
            pe.wait_ge(y_end_set, 1)

            def column_group(gg, p, x, slices, blocks, landed_by):
                pe.wait_ge(sum_copied, gg + 1)
                for cg in range(CG):
                    landed_by(cg)
                    m = slices[:, cg, :].rearrange("p (b c d) -> p b c d", b=GB, d=BLK)
                    for ci in range(CI):
                        c = cg * CI + ci
                        o = ps[F * (c % 2):F * (c % 2) + F, BANK[p], 0:blocks * BLK].rearrange("p (b d) -> p b d", d=BLK)
                        last = pe.matmul(o, x[:, c, :], m[:, 0:blocks, ci, :], start=(c < 2), stop=(c >= CH - 2))
                    last.then_inc(slice_used, 1)

            def streamed(use):
                return lambda cg: pe.wait_ge(landed[cg], 16 * use + 16)

            def by_nodes(k, rhs, a, b):
                pe.wait_ge(sum_copied, GROUPS * (k + 1) + 2 if b == CH else GROUPS * (k + 1))
                for c in range(a, b):
                    last = pe.matmul(ps[:, 2 + c // 8, F * (c % 8):F * (c % 8) + F], y_t[:, c * PC:c * PC + P], rhs, start=True, stop=True)
                return last

            with pe.Fori(0, (GROUPS - 1) // 2) as it:
                for p in range(2):
                    column_group(2 * it + p, p, x1, ring, GB, streamed(2 * it + p))
            pe.wait_ge(own_read, 1)
            by_nodes(0, wa2_t[:, :], 0, FIRST)
            column_group(GROUPS - 1, GROUPS - 1, x1, ring, LASTB, streamed(GROUPS - 1))
            by_nodes(0, wa2_t[:, :], FIRST, CH).then_inc(node_put, 1)
            with pe.Fori(1, KP) as k:
                pe.wait_ge(x_ready, k + 1)
                for p, g in enumerate(ORDER):
                    gg = GROUPS * k + p
                    if g == GROUPS - 1:
                        by_nodes(k, ident2[:, :], 0, FIRST)
                    if p in STREAMED:
                        column_group(gg, p, cur, ring, LASTB if g == GROUPS - 1 else GB, streamed(GROUPS + len(STREAMED) * (k - 1) + STREAMED.index(p)))
                    else:
                        column_group(gg, p, cur, resident[:, CG * g:CG * g + CG, :], GB,
                                     lambda cg: pe.wait_ge(resident_landed[g], 16 * CG) if cg == 0 else None)
                by_nodes(k, ident2[:, :], FIRST, CH).then_inc(node_put, 1)
            def fc_place(c):
                return ps[:, (0, 1, 6, 7)[c // 8], F * (c % 8):F * (c % 8) + F]

            pe.wait_ge(sum_copied, GROUPS * KP + 2)
            for c in range(CH):
                pe.matmul(fc_place(c), y_t[:, c * PC:c * PC + P], fc_t[:, 0, :], start=(c % 8 == 0), stop=False, skip_group_check=True)

            def chunks(u):
                return range(4 * (u % 7), min(4 * (u % 7) + 4, CH))

            pe.wait_ge(x_ready, KP + 1)
            for u in range(15):
                if u < 14:
                    if u % 7 == 0:
                        pe.wait_ge(feats_ready, 2 * (u // 7) + 2)
                    if u >= 2:
                        pe.wait_ge(ft_copied, u - 1)
                    for c in chunks(u):
                        last = pe.transpose(ps[:, 2 + u % 2, P * (c % 4):P * (c % 4) + P], feats[:, u // 7, c, :, :].rearrange(FLAT), ident[:, :])
                    last.then_inc(ft_put, 1)
                if u:
                    w = u - 1
                    pe.wait_ge(ft_copied, w + 1)
                    for c in chunks(w):
                        last = pe.matmul(fc_place(c), feats_t[:, w % 2, P * (c % 4):P * (c % 4) + P], fc_t[:, 1 + w // 7, :],
                                         start=False, stop=(w >= 7), skip_group_check=True)
                    last.then_inc(fc_put, 1)


_INS = [("x", "x"), ("src", "src"), ("dst", "dst"), ("edge_type_16", "type"), ("edge_weight", "weight"),
        ("L0_gnn_weight", "rel_w"), ("L1_gnn_W", "l1_w"), ("L1_gnn_b", "l1_b"), ("L3_gnn_fc_w", "fc_w"),
        ("L3_gnn_bias", "fc_b"), ("L3_gnn_prelu_a", "prelu_a")]


def kernel(**inputs):
    import numpy as np
    import concourse.bacc as bacc
    from concourse import mybir as _mybir
    from concourse.bass_utils import run_bass_kernel_spmd as run

    nc = bacc.Bacc("TRN2", target_bir_lowering=False, num_devices=1)
    arrays, args = {}, []
    for name, short in _INS:
        a = np.ascontiguousarray(inputs[name])
        if a.ndim == 0:
            a = a.reshape(1)
        arrays[short] = a
        args.append(nc.dram_tensor(short, a.shape, _mybir.dt.from_np(a.dtype), kind="ExternalInput").ap())
    out = nc.dram_tensor("out", (N, F), F32, kind="ExternalOutput").ap()
    build(nc, *args, out)
    r = run(nc, [arrays], core_ids=[0])
    return r.results[0]["out"]
```
